# Optimizing a Trainium2 kernel written in Bass

```python
import numpy as np
import jax
import jax.numpy as jnp

def _softmax(x, axis=-1):
    return jax.nn.softmax(x, axis=axis)
def _gelu(x):
    return jax.nn.gelu(x, approximate=True)
def _silu(x):
    return jax.nn.silu(x)
def _sigmoid(x):
    return jax.nn.sigmoid(x)
def _layernorm(x, axis=-1, eps=1e-5):
    m = jnp.mean(x, axis=axis, keepdims=True)
    v = jnp.var(x, axis=axis, keepdims=True)
    return (x - m) / jnp.sqrt(v + eps)
def _scatter_add(tgt, idx, src, axis=0):
    return tgt.at[idx].add(src)
def _segment_sum(src, seg, n):
    return jax.ops.segment_sum(src, seg, n)

kernel_name = 'mk_conv_seq_d2_conv_nchw512_6b88d6'

def setup_inputs(seed: int = 0):
    np.random.seed(seed)
    _w = jnp.asarray
    def _rec_inputs():
        import jax
        import jax.numpy as jnp
        _gk = jax.random.key(seed)
        x = -0.0002928 + 1 * jax.random.normal(jax.random.fold_in(_gk, 1), (8, 512, 32, 32), jnp.float32)
        return x
    x = _rec_inputs()
    def _L0_conv_setup():
        import jax, jax.numpy as jnp
        import numpy as np
        N, C, H, W = (8, 512, 32, 32)
        NH = 8
        CH = C // NH
        EPS = 1e-05
        key = jax.random.key(seed)
        ks = jax.random.split(key, 4)
        x = jax.random.normal(ks[0], (N, C, H, W), dtype=jnp.float32)
        gn_weight = jnp.ones((C,), dtype=jnp.float32)
        gn_bias = jnp.zeros((C,), dtype=jnp.float32)
        qkv_w = jax.random.normal(ks[1], (3 * C, C), dtype=jnp.float32) * C ** (-0.5)
        qkv_b = jnp.zeros((3 * C,), dtype=jnp.float32)
        out_w = jax.random.normal(ks[2], (C, C), dtype=jnp.float32) * C ** (-0.5)
        out_b = jnp.zeros((C,), dtype=jnp.float32)
        return {'x': x, 'gn_weight': gn_weight, 'gn_bias': gn_bias, 'qkv_w': qkv_w, 'qkv_b': qkv_b, 'out_w': out_w, 'out_b': out_b}
    _L0_conv_all = _L0_conv_setup()
    _L0_conv_in = {k: v for k, v in _L0_conv_all.items() if k in ('gn_weight', 'gn_bias', 'qkv_w', 'qkv_b', 'out_w', 'out_b', )}
    del _L0_conv_all

    def _L1_conv_setup():
        import jax, jax.numpy as jnp
        import numpy as np
        DIM = 8
        EPS = 1e-15
        GROUPS_PW = 192

        def _conv(x, w, groups=1, pad=0):
            return jax.lax.conv_general_dilated(x, w, window_strides=(1, 1), padding=[(pad, pad), (pad, pad)], dimension_numbers=('NCHW', 'OIHW', 'NCHW'), feature_group_count=groups)
        key = jax.random.key(seed)
        k0, k1, k2, k3, k4 = jax.random.split(key, 5)
        B, C, H, W = (4, 512, 64, 64)
        td = 512
        x = jax.random.normal(k0, (B, C, H, W), jnp.float32)
        w_qkv = jax.random.normal(k1, (3 * td, C, 1, 1), jnp.float32) * 0.05
        w_dw = jax.random.normal(k2, (3 * td, 1, 5, 5), jnp.float32) * 0.05
        w_pw = jax.random.normal(k3, (3 * td, 3 * td // GROUPS_PW, 1, 1), jnp.float32) * 0.05
        w_proj = jax.random.normal(k4, (C, 2 * td, 1, 1), jnp.float32) * 0.05
        return {'x': x, 'w_qkv': w_qkv, 'w_dw': w_dw, 'w_pw': w_pw, 'w_proj': w_proj}
    _L1_conv_all = _L1_conv_setup()
    _L1_conv_in = {k: v for k, v in _L1_conv_all.items() if k in ('w_qkv', 'w_dw', 'w_pw', 'w_proj', )}
    del _L1_conv_all

    return {
        "x": x,
        "L0_conv_gn_weight": _L0_conv_in["gn_weight"],
        "L0_conv_gn_bias": _L0_conv_in["gn_bias"],
        "L0_conv_qkv_w": _L0_conv_in["qkv_w"],
        "L0_conv_qkv_b": _L0_conv_in["qkv_b"],
        "L0_conv_out_w": _L0_conv_in["out_w"],
        "L0_conv_out_b": _L0_conv_in["out_b"],
        "L1_conv_w_qkv": _L1_conv_in["w_qkv"],
        "L1_conv_w_dw": _L1_conv_in["w_dw"],
        "L1_conv_w_pw": _L1_conv_in["w_pw"],
        "L1_conv_w_proj": _L1_conv_in["w_proj"],
    }

def reference(x, L0_conv_gn_weight, L0_conv_gn_bias, L0_conv_qkv_w, L0_conv_qkv_b, L0_conv_out_w, L0_conv_out_b, L1_conv_w_qkv, L1_conv_w_dw, L1_conv_w_pw, L1_conv_w_proj):
    import jax
    import jax.numpy as jnp
    def _L0_conv_ref(x, gn_weight, gn_bias, qkv_w, qkv_b, out_w, out_b):
        import jax, jax.numpy as jnp
        import numpy as np
        N, C, H, W = (8, 512, 32, 32)
        NH = 8
        CH = C // NH
        EPS = 1e-05
        n, c, h, w = x.shape
        L = h * w
        mean = jnp.mean(x, axis=(1, 2, 3), keepdims=True)
        var = jnp.var(x, axis=(1, 2, 3), keepdims=True)
        u = (x - mean) * jax.lax.rsqrt(var + EPS)
        u = u * gn_weight[None, :, None, None] + gn_bias[None, :, None, None]
        qkv = jnp.einsum('oc,nchw->nohw', qkv_w, u) + qkv_b[None, :, None, None]
        qkv = qkv.reshape(n, 3, NH, CH, L).transpose(0, 1, 2, 4, 3)
        q, k, v = (qkv[:, 0], qkv[:, 1], qkv[:, 2])
        scale = CH ** (-0.25)
        att = jnp.einsum('nhlc,nhLc->nhlL', q * scale, k * scale)
        att = jax.nn.softmax(att, axis=3)
        y = jnp.einsum('nhlL,nhLc->nhlc', att, v)
        y = y.transpose(0, 1, 3, 2).reshape(n, c, h, w)
        out = x + jnp.einsum('oc,nchw->nohw', out_w, y) + out_b[None, :, None, None]
        return out

    def _L1_conv_ref(x, w_qkv, w_dw, w_pw, w_proj):
        import jax, jax.numpy as jnp
        import numpy as np
        DIM = 8
        EPS = 1e-15
        GROUPS_PW = 192

        def _conv(x, w, groups=1, pad=0):
            return jax.lax.conv_general_dilated(x, w, window_strides=(1, 1), padding=[(pad, pad), (pad, pad)], dimension_numbers=('NCHW', 'OIHW', 'NCHW'), feature_group_count=groups)
        qkv = _conv(x, w_qkv)
        agg = _conv(_conv(qkv, w_dw, groups=w_dw.shape[0], pad=2), w_pw, groups=GROUPS_PW)
        qkv = jnp.concatenate([qkv, agg], axis=1)
        B, _, H, W = qkv.shape
        qkv = qkv.reshape(B, -1, 3 * DIM, H * W)
        q = jax.nn.relu(qkv[:, :, :DIM])
        k = jax.nn.relu(qkv[:, :, DIM:2 * DIM])
        v = qkv[:, :, 2 * DIM:]
        v = jnp.pad(v, ((0, 0), (0, 0), (0, 1), (0, 0)), constant_values=1.0)
        vk = jnp.einsum('bhdn,bhen->bhde', v, k)
        out = jnp.einsum('bhde,bhen->bhdn', vk, q)
        out = out[:, :, :-1] / (out[:, :, -1:] + EPS)
        out = out.reshape(B, -1, H, W)
        return x + _conv(out, w_proj)

    def _gn(v, G=32, eps=1e-5):
        B_, C_, H_, W_ = v.shape
        g = v.reshape(B_, G, C_ // G, H_, W_)
        m = jnp.mean(g, axis=(2, 3, 4), keepdims=True)
        s = jnp.var(g, axis=(2, 3, 4), keepdims=True)
        return ((g - m) / jnp.sqrt(s + eps)).reshape(v.shape)

    def _ln_c(v, eps=1e-6):
        m = jnp.mean(v, axis=1, keepdims=True)
        s = jnp.var(v, axis=1, keepdims=True)
        return (v - m) / jnp.sqrt(s + eps)

    def _ln_t(v, eps=1e-5):
        m = jnp.mean(v, axis=-1, keepdims=True)
        s = jnp.var(v, axis=-1, keepdims=True)
        return (v - m) / jnp.sqrt(s + eps)

    def _to_tokens(v):
        B_, C_, H_, W_ = v.shape
        return v.reshape(B_, C_, H_ * W_).transpose(0, 2, 1)
    def _from_tokens(t, like):
        B_, C_, H_, W_ = like.shape
        return t.transpose(0, 2, 1).reshape(B_, C_, H_, W_)

    x = _L0_conv_ref(x, L0_conv_gn_weight, L0_conv_gn_bias, L0_conv_qkv_w, L0_conv_qkv_b, L0_conv_out_w, L0_conv_out_b)
    x = _L1_conv_ref(x, L1_conv_w_qkv, L1_conv_w_dw, L1_conv_w_pw, L1_conv_w_proj)
    return x


_drawn_inputs = setup_inputs


def setup_inputs(seed=0):
    import zlib

    import numpy as np

    out = dict(_drawn_inputs(seed))
    spreads = {'L0_conv_gn_weight': (1.0, 0.2),
     'L0_conv_gn_bias': (0.0, 0.1),
     'L0_conv_qkv_b': (0.0, 0.1),
     'L0_conv_out_b': (0.0, 0.1)}
    factors = {'L1_conv_w_dw': 8.0, 'L1_conv_w_pw': 7.929}
    for name, (base, spread) in spreads.items():
        noise = np.random.default_rng([zlib.crc32(name.encode()), seed]).standard_normal(out[name].shape)
        drawn = base * np.exp(spread * noise) if base else spread * noise
        out[name] = jnp.asarray(drawn.astype(out[name].dtype))
    for name, factor in factors.items():
        out[name] = (out[name] * factor).astype(out[name].dtype)
    return out
```

```python
from contextlib import ExitStack

import numpy as np
import concourse.bass as bass
from concourse import mybir

P = 128
F32 = mybir.dt.float32
F32R = mybir.dt.float32r
ALU = mybir.AluOpType
ACT = mybir.ActivationFunctionType
AX_X = mybir.AxisListType.X

NB, C, H, W = 8, 512, 32, 32
L = H * W
CB = C // P
NHEAD, CH = 8, 64
PAIRS = NHEAD // 2
QB = L // P
GN_EPS = 1e-5
TAPS = 5
PAD = TAPS // 2
HP = H + 2 * PAD
DIM = 8
HEADS_SET = P // DIM
SETS = C // P
BLOCKS = 3 * SETS
ATT_EPS = 1e-15
HALF = 512
UNITS = NHEAD * QB
NW = P + HEADS_SET
FILL0 = 6

TAP_STEPS = TAPS * TAPS
CONV_STEPS = TAP_STEPS + 1
CHAIN = [1 if i < 3 else (0 if i % 2 else 1) for i in range(TAP_STEPS)]
CHUNK = [6, 5, 5, 5, 5]


def layer1_chunks():
    chunks = []
    for m in range(BLOCKS + 1):
        for r in range(len(CHUNK)):
            groups = []
            j, t = divmod(m, 3)
            if r == 0 and m > 0:
                groups += [("PW", m - 1, h) for h in range(2)]
            if r == 1 and m + 1 < BLOCKS:
                groups += [("P1", m + 1, h) for h in range(2)]
            if m < BLOCKS and t == 1:
                if r == 0:
                    groups += [("TK", j, h) for h in range(2)]
                if r == 2:
                    groups += [("TV", j, h) for h in range(2)]
                if r == 3:
                    groups += [("VK", 0, j)]
                if r == 4:
                    groups += [("NUM", 0, j, g) for g in range(3)]
            if m < BLOCKS and t == 2 and r == 1:
                groups += [("TB", 0, j, h) for h in range(2)]
            if t == 0 and m > 0:
                if r == 2:
                    groups += [("VK", 1, j - 1)]
                if r == 3:
                    groups += [("NUM", 1, j - 1, g) for g in range(3)]
                if r == 4:
                    groups += [("TB", 1, j - 1, h) for h in range(2)]
            lo = sum(CHUNK[:r])
            steps = [("CONV", m, i) for i in range(lo, lo + CHUNK[r])] if m < BLOCKS else []
            if groups or steps:
                chunks.append((groups, steps))
    return chunks


def timeline(l0, l1):
    chunks = layer1_chunks() if l1 else []
    total = len(chunks)
    done = [0]
    out = []

    def take(upto):
        part = ([], [])
        while done[0] < min(upto, total):
            g, s = chunks[done[0]]
            part[0].extend(g)
            part[1].extend(s)
            done[0] += 1
        return part

    if l1:
        out += [("P1", 0, 0), ("P1", 0, 1)]
    if l0:
        out += [("STATS",), ("MEAN",), ("VAR",)]
        first = [("V", i) for i in range(QB)] + [("QK", 0, t, h) for t in range(2) for h in range(2)]
        for i, step in enumerate(first):
            out.append(step)
            g, s = take((i + 1) * FILL0 // len(first))
            out += g + s
        out += [("S", 0), ("MAX", 0), ("EXP", 0)]
        for n in range(UNITS):
            g, s = take(FILL0 + -(-(n + 1) * (total - FILL0) // (UNITS - 1)))
            k = (len(s) + 1) // 2
            last_of_pair = n % (2 * QB) == 2 * QB - 1
            nxt = n + 1 < UNITS
            if nxt and last_of_pair:
                out += [("QK", (n + 1) // (2 * QB), t, h) for t in range(2) for h in range(2)]
            if n % 4 == 3:
                out.append(("RECIP", n // 4))
            if nxt:
                out += [("S", n + 1), ("MAX", n + 1)]
            out += s[:k] + g
            if nxt:
                out.append(("EXP", n + 1))
            if n % 4 == 0 and n > 0:
                out.append(("AV", n // 4 - 1))
            out.append(("T", n))
            out += s[k:]
        out.append(("AV", UNITS // 4 - 1))
    else:
        g, s = take(0)
    while done[0] < total:
        g, s = take(done[0] + 1)
        out += g + s
    if l1:
        out += [("PROJ", i) for i in range(2 * CB)]
    if l0:
        out += [("OUT", i) for i in range(2 * CB)]
    return out


GROUPS = ("P1", "MEAN", "VAR", "V", "QK", "PW", "TK", "TV", "VK", "NUM", "TB", "AV", "PROJ", "OUT")


def build(nc, x, w0qk, w0v, w0out, w1, wproj, pw, dw, gnw, gnb, qk_bias, v_bias, out_bias,
          identity, block_mask, head_mask, ones, out):
    STEPS = {f: timeline(*f) for f in ((True, False), (True, True), (False, True))}
    INDEX = {}
    for f, steps in STEPS.items():
        INDEX[f] = {s: i for i, s in enumerate([s for s in steps if s[0] in GROUPS])}
    G0, G1 = len(INDEX[True, False]), len(INDEX[False, True])
    assert len(INDEX[True, True]) == G0 + G1 and G0 % 2 == 0 and G1 % 2 == 0
    FIRST, BOTH, LAST = (True, False), (True, True), (False, True)

    ctx = ExitStack()
    with ctx:
        def sb(name, shape, dt=F32):
            return ctx.enter_context(nc.sbuf_tensor(name, shape, dt))

        def psum(name, shape):
            return ctx.enter_context(nc.psum_tensor(name, shape, F32))

        def sem(name):
            return ctx.enter_context(nc.semaphore(name))

        class Signal:

            def __init__(self, name, l0, l1, by=1):
                self.sem, self.l0, self.l1, self.by = sem(name), l0, l1, by

            def value(self, it, n):
                if isinstance(it, int):
                    k = self.l0 * min(it, NB) + self.l1 * max(it - 1, 0)
                    return (k + n) * self.by
                return it * ((self.l0 + self.l1) * self.by) + (n - self.l1) * self.by

        def positive(v):
            return not (isinstance(v, int) and v <= 0)

        w_small = sb("w_small", [P, CB, C])
        w0qk_sb = sb("w0qk_sb", [P, CB, 2, P])
        w1_sb = sb("w1_sb", [P, CB, 3, P])
        pw_dense = sb("pw_dense", [P, BLOCKS, DIM])
        pw_bd = sb("pw_bd", [P, BLOCKS, P])
        dw_sb = sb("dw_sb", [P, BLOCKS, TAPS * TAPS])
        gnw_sb = sb("gnw_sb", [P, CB])
        gnb_sb = sb("gnb_sb", [P, CB])
        qkb_sb = sb("qkb_sb", [P, NHEAD, 2])
        vb_sb = sb("vb_sb", [P, PAIRS])
        outb_sb = sb("outb_sb", [P, CB])
        outb2 = sb("outb2", [P, CB])
        ident = sb("ident", [P, P])
        bdmask = sb("bdmask", [P, P])
        hmask = sb("hmask", [P, HEADS_SET])
        mean_w = sb("mean_w", [P, P])
        u = sb("u", [P, CB, L])
        q_st = sb("q_st", [P, 2, L], F32R)
        k_st = sb("k_st", [P, 2, 2, L], F32R)
        vy = sb("vy", [P, PAIRS + 1, L])
        probs = [sb(f"probs{i}", [P, L]) for i in range(2)]
        pt = sb("pt", [P, 2, QB, 2 * P])
        x1 = sb("x1", [P, CB, L])
        pads = [sb(f"pad{i}", [P, HP, HP]) for i in range(3)]
        acc = [sb(f"acc{i}", [P, H, W]) for i in range(2)]
        side = sb("side", [P, H, W])
        q_orig = sb("q_orig", [P, L])
        q_agg = sb("q_agg", [P, L])
        kv_raw = sb("kv_raw", [P, L])
        k_t = sb("k_t", [P, QB, P])
        v_t = sb("v_t", [P, QB, P + 1])
        vk = sb("vk", [P, NW])
        den = sb("den", [P, 2, 2, 3 * HEADS_SET])
        num_t = sb("num_t", [P, QB, P])
        feat = sb("feat", [P, 2 * SETS, L])
        row_sum = sb("row_sum", [P, 16])
        inv_sum = sb("inv_sum", [P, 2, 4])
        inv_wide = sb("inv_wide", [P, 4, CH])
        inv_q = sb("inv_q", [P, 2 * P])
        neg_max = sb("neg_max", [P, 4])
        exp_bias = sb("exp_bias", [P, 4])
        bn6 = sb("bn6", [P, 2 * CB, 6])
        mv = sb("mv", [P, 2])
        gn = sb("gn", [P, 7])
        gn_a = sb("gn_a", [P, CB])
        gn_nb = sb("gn_nb", [P, CB])
        wproj_sb = pt[:, :, :, :].rearrange("p a b c -> p (a b c)").rearrange("p (b n) -> p b n", b=2 * SETS)
        x_res = [probs[0][:, i * HALF:(i + 1) * HALF] for i in range(2)]
        y_out = [probs[1][:, i * HALF:(i + 1) * HALF] for i in range(2)]

        scores = [psum(f"scores{i}", [P, L]) for i in range(2)]
        pt_ps = psum("pt_ps", [P, QB, P])
        bank = [psum(f"bank{i}", [P, HALF]) for i in range(2)]

        const_in = sem("const_in")
        w0out_pre = sem("w0out_pre")
        setup_dve = sem("setup_dve")
        setup_pe = sem("setup_pe")
        x_in = Signal("x_in", 1, 0, 16)
        w0v_in = Signal("w0v_in", 1, 0, 16)
        w0qk_in = Signal("w0qk_in", PAIRS, 0, 16)
        w0out_in = Signal("w0out_in", 1, 0, 16)
        w1_in = Signal("w1_in", 0, SETS, 16)
        wproj_in = Signal("wproj_in", 0, 1, 16)
        x_res_in = [Signal(f"x_res_in{i}", CB, 0, 16) for i in range(2)]
        out_sent = [Signal(f"out_sent{i}", 0, CB, 16) for i in range(2)]
        product = Signal("product", G0, G1)
        emptied = [Signal(f"emptied{i}", G0 // 2, G1 // 2) for i in range(2)]
        scores_full = Signal("scores_full", UNITS, 0)
        max_done = Signal("max_done", UNITS, 0)
        bias_done = Signal("bias_done", UNITS, 0)
        exp_done = Signal("exp_done", UNITS, 0)
        pt_full = Signal("pt_full", UNITS, 0)
        pt_copied = Signal("pt_copied", UNITS, 0)
        inv_done = Signal("inv_done", UNITS // 4, 0)
        wide_done = Signal("wide_done", UNITS // 4, 0)
        inv_q_done = Signal("inv_q_done", UNITS // 4, 0)
        high_done = Signal("high_done", 4 * PAIRS, 0)
        twice_done = Signal("twice_done", 2 * PAIRS, 0)
        stats_done = Signal("stats_done", 2, 0)
        var_done = Signal("var_done", 1, 0)
        std_done = Signal("std_done", 1, 0)
        u_ready = Signal("u_ready", 1, 0)
        conv_step = Signal("conv_step", 0, BLOCKS * CONV_STEPS)
        LINKS0, LINKS1 = 5, 2 * SETS * 3 * 2
        link_done = Signal("link_done", LINKS0, LINKS1)

        def products(f, it, step):
            return product.value(it, INDEX[f][step] + 1)

        def copies(f, it, *steps):
            last = {}
            for g in sorted(INDEX[f][s] for s in steps):
                last[g % 2] = g
            return [(b, emptied[b].value(it, g // 2 + 1)) for b, g in last.items()]

        block = ctx.enter_context(nc.Block())

        @block.sync
        def _(sp):
            for dst, src in ((pw_dense, pw), (dw_sb, dw), (gnw_sb, gnw), (gnb_sb, gnb), (qkb_sb, qk_bias),
                             (vb_sb, v_bias), (outb_sb, out_bias), (ident, identity), (bdmask, block_mask),
                             (hmask, head_mask), (mean_w, ones)):
                sp.dma_start(dst[:], src).then_inc(const_in, 16)

            def load_x(it):
                src = x[bass.ds(it, 1)] if not isinstance(it, int) else x[it:it + 1]
                sp.dma_start(u[:], src.rearrange("a (k p) t -> p (a k) t", p=P)).then_inc(x_in.sem, 16)

            def load_w0qk(j):
                sp.dma_start(w0qk_sb[:], w0qk[j]).then_inc(w0qk_in.sem, 16)

            def load_w1(j):
                sp.dma_start(w1_sb[:], w1[j]).then_inc(w1_in.sem, 16)

            load_x(0)
            sp.dma_start(w_small[:], w0v).then_inc(w0v_in.sem, 16)
            load_w0qk(0)
            load_w1(0)
            sp.dma_start(wproj_sb[:, 0:CB, :], w0out).then_inc(w0out_pre, 16)

            def iteration(it, f, more):
                l0, l1 = f
                if l0:
                    sp.wait_ge(product.sem, products(f, it, ("V", QB - 1)))
                    sp.dma_start(w_small[:], w0out).then_inc(w0out_in.sem, 16)
                for j in range(PAIRS):
                    if l0 and (j + 1 < PAIRS or more):
                        sp.wait_ge(product.sem, products(f, it, ("QK", j, 1, 1)))
                        load_w0qk((j + 1) % PAIRS)
                        if j + 1 == PAIRS:
                            load_x(it + 1)
                    if l1 and (j + 1 < SETS or l0):
                        sp.wait_ge(product.sem, products(f, it, ("P1", 3 * j + 2, 1)))
                        load_w1((j + 1) % SETS)
                if l1:
                    if l0:
                        sp.wait_ge(product.sem, products(f, it, ("AV", UNITS // 4 - 1)))
                    sp.dma_start(wproj_sb[:], wproj).then_inc(wproj_in.sem, 16)
                if l0:
                    for i in range(2 * CB):
                        if i < 2:
                            sp.wait_ge(pt_full.sem, pt_full.value(it, UNITS))
                        else:
                            for which, count in copies(f, it, ("OUT", i - 2)):
                                sp.wait_ge(emptied[which].sem, count)
                        ob, h = divmod(i, 2)
                        src = x[bass.ds(it, 1)] if not isinstance(it, int) else x[it:it + 1]
                        src = src[:, ob * P:(ob + 1) * P, h * HALF:(h + 1) * HALF]
                        sp.dma_start(x_res[i % 2], src.rearrange("a p t -> (a p) t"))\
                            .then_inc(x_res_in[i % 2].sem, 16)
                    if more:
                        sp.wait_ge(product.sem, products(f, it, ("OUT", 2 * CB - 1)))
                        sp.dma_start(w_small[:], w0v).then_inc(w0v_in.sem, 16)

            iteration(0, FIRST, True)
            with sp.Fori(1, NB - 1) as it:
                iteration(it, BOTH, True)
            iteration(NB - 1, BOTH, False)
            iteration(NB, LAST, False)

        @block.tensor
        def _(pe):
            mm = nc.tensor.matmul
            pe.wait_ge(const_in, 16 * 11)
            pe.wait_ge(w0out_pre, 16)
            for ob in range(CB):
                for j in range(PAIRS):
                    last = mm(scores[0][:, ob:ob + 1], wproj_sb[:, j, ob * P:(ob + 1) * P], vb_sb[:, j:j + 1],
                              start=(j == 0), stop=(j == PAIRS - 1))
            last.then_inc(setup_pe, 1)
            pe.wait_ge(setup_dve, 3)

            def group(it, f, step):
                g = INDEX[f][step]
                b = bank[g % 2]
                if positive(emptied[g % 2].value(it, g // 2)):
                    pe.wait_ge(emptied[g % 2].sem, emptied[g % 2].value(it, g // 2))
                kind = step[0]
                if kind in ("MEAN", "VAR"):
                    pe.wait_ge(stats_done.sem, stats_done.value(it, 1 if kind == "MEAN" else 2))
                    rhs = mv[:, 0:1] if kind == "MEAN" else gn[:, 1:2]
                    last = mm(b[:, 0:1], mean_w[:], rhs, start=True, stop=True)
                elif kind == "V":
                    tb = step[1]
                    if tb == 0:
                        pe.wait_ge(u_ready.sem, u_ready.value(it, 1))
                        pe.wait_ge(w0v_in.sem, w0v_in.value(it, 1))
                    for k in range(CB):
                        last = mm(b[:], u[:, k, tb * P:(tb + 1) * P], w_small[:, k, :],
                                  start=(k == 0), stop=(k == CB - 1))
                elif kind == "QK":
                    _, j, t, h = step
                    if t == 0 and h == 0:
                        pe.wait_ge(w0qk_in.sem, w0qk_in.value(it, j + 1))
                    for k in range(CB):
                        last = mm(b[:], w0qk_sb[:, k, t, :], u[:, k, h * HALF:(h + 1) * HALF],
                                  start=(k == 0), stop=(k == CB - 1))
                elif kind == "AV":
                    c = step[1]
                    j = c // 4
                    pe.wait_ge(wide_done.sem, wide_done.value(it, c + 1))
                    pe.wait_ge(pt_copied.sem, pt_copied.value(it, 4 * c + 4))
                    if c == 0:
                        for which, count in copies(f, it, ("V", QB - 2), ("V", QB - 1)):
                            pe.wait_ge(emptied[which].sem, count)
                    for q in range(2):
                        nc.tensor.transpose(b[:, (2 + q) * P:(3 + q) * P],
                                            inv_wide[:, 2 * q:2 * q + 2, :].rearrange("p a c -> p (a c)"), ident[:])
                    for kb in range(QB):
                        for hd in range(2):
                            last = mm(b[hd * CH:(hd + 1) * CH, 0:2 * P],
                                      vy[:, j + 1, kb * P + hd * CH:kb * P + (hd + 1) * CH],
                                      pt[:, hd, kb, :], start=(kb == 0), stop=(kb == QB - 1))
                elif kind == "OUT":
                    ob, h = divmod(step[1], 2)
                    if step[1] == 0:
                        pe.wait_ge(w0out_in.sem, w0out_in.value(it, 1))
                        for which, count in copies(f, it, ("AV", UNITS // 4 - 2), ("AV", UNITS // 4 - 1)):
                            pe.wait_ge(emptied[which].sem, count)
                    for j in range(PAIRS):
                        last = mm(b[:], w_small[:, j, ob * P:(ob + 1) * P], vy[:, j, h * HALF:(h + 1) * HALF],
                                  start=(j == 0), stop=(j == PAIRS - 1))
                elif kind == "P1":
                    _, m, h = step
                    j, t = divmod(m, 3)
                    if h == 0 and t == 0:
                        pe.wait_ge(w1_in.sem, w1_in.value(it, j + 1))
                    if h == 0 and m == 0:
                        for i in range(2):
                            pe.wait_ge(emptied[i].sem, emptied[i].value(it, 0))
                    for k in range(CB):
                        last = mm(b[:], w1_sb[:, k, t, :], x1[:, k, h * HALF:(h + 1) * HALF],
                                  start=(k == 0), stop=(k == CB - 1))
                elif kind == "PW":
                    _, m, h = step
                    if h == 0:
                        pe.wait_ge(conv_step.sem, conv_step.value(it, (m + 1) * CONV_STEPS))
                    a = acc[m % 2][:].rearrange("p a b -> p (a b)")
                    if m % 3 == 0:
                        last = mm(b[:], pw_bd[:, m, :], a[:, h * HALF:(h + 1) * HALF], start=True, stop=True)
                    else:
                        for i in range(4):
                            tb = 4 * h + i
                            last = mm(b[:, i * P:(i + 1) * P], a[:, tb * P:(tb + 1) * P], pw_bd[:, m, :],
                                      start=True, stop=True)
                elif kind in ("TK", "TV"):
                    _, j, h = step
                    for which, count in copies(f, it, ("P1", 3 * j + (1 if kind == "TK" else 2), h)):
                        pe.wait_ge(emptied[which].sem, count)
                    for i in range(4):
                        tb = 4 * h + i
                        last = nc.tensor.transpose(b[:, i * P:(i + 1) * P], kv_raw[:, tb * P:(tb + 1) * P], ident[:])
                elif kind == "VK":
                    _, s, j = step
                    if s == 0:
                        for which, count in copies(f, it, *[(kind, j, h) for kind in ("TK", "TV") for h in range(2)]):
                            pe.wait_ge(emptied[which].sem, count)
                    else:
                        for which, count in copies(f, it, *[("PW", 3 * j + t, h) for t in (1, 2) for h in range(2)]):
                            pe.wait_ge(emptied[which].sem, count)
                    for tb in range(QB):
                        last = mm(b[:, 0:P + 1], k_t[:, tb, :], v_t[:, tb, :], start=(tb == 0), stop=(tb == QB - 1))
                elif kind == "NUM":
                    _, s, j, g3 = step
                    if g3 == 0:
                        for which, count in copies(f, it, ("VK", s, j), *[("P1" if s == 0 else "PW", 3 * j, h) for h in range(2)]):
                            pe.wait_ge(emptied[which].sem, count)
                    q = q_orig if s == 0 else q_agg
                    for i, tb in enumerate(range(3 * g3, min(QB, 3 * g3 + 3))):
                        last = mm(b[:, i * NW:(i + 1) * NW], q[:, tb * P:(tb + 1) * P], vk[:], start=True, stop=True)
                elif kind == "TB":
                    _, s, j, h = step
                    for which, count in copies(f, it, *[("NUM", s, j, g3) for g3 in ((0, 1) if h == 0 else (2,))]):
                        pe.wait_ge(emptied[which].sem, count)
                    for i in range(4):
                        last = nc.tensor.transpose(b[:, i * P:(i + 1) * P], num_t[:, 4 * h + i, :], ident[:])
                elif kind == "PROJ":
                    ob, h = divmod(step[1], 2)
                    if step[1] == 0:
                        pe.wait_ge(wproj_in.sem, wproj_in.value(it, 1))
                        for which, count in copies(f, it, *[("TB", s, j, hh) for s in range(2) for j in range(SETS) for hh in range(2)]):
                            pe.wait_ge(emptied[which].sem, count)
                    for k in range(2 * SETS):
                        last = mm(b[:], wproj_sb[:, k, ob * P:(ob + 1) * P], feat[:, k, h * HALF:(h + 1) * HALF],
                                  start=(k == 0), stop=(k == 2 * SETS - 1))
                last.then_inc(product.sem, 1)

            def iteration(it, f):
                for step in STEPS[f]:
                    if step[0] in GROUPS:
                        group(it, f, step)
                    elif step[0] == "S":
                        n = step[1]
                        j, qb, hd = n // (2 * QB), n // 2 % QB, n % 2
                        if positive(exp_done.value(it, n - 1)):
                            pe.wait_ge(exp_done.sem, exp_done.value(it, n - 1))
                        if n % (2 * QB) == 0:
                            for which, count in copies(f, it, *[("QK", j, t, h) for t in range(2) for h in range(2)]):
                                pe.wait_ge(emptied[which].sem, count)
                            pe.wait_ge(twice_done.sem, twice_done.value(it, 2 * j + 2))
                        for h in range(2):
                            for part in range(2):
                                last = mm(scores[hd][:, h * HALF:(h + 1) * HALF], q_st[:, hd, qb * P:(qb + 1) * P],
                                          k_st[:, hd, part, h * HALF:(h + 1) * HALF],
                                          start=(part == 0), stop=(part == 1))
                        last.then_inc(scores_full.sem, 1)
                    elif step[0] == "T":
                        n = step[1]
                        pe.wait_ge(exp_done.sem, exp_done.value(it, n + 1))
                        if positive(pt_copied.value(it, n)):
                            pe.wait_ge(pt_copied.sem, pt_copied.value(it, n))
                        for kb in range(QB):
                            last = nc.tensor.transpose(pt_ps[:, kb, :], probs[n % 2][:, kb * P:(kb + 1) * P], ident[:])
                        last.then_inc(pt_full.sem, 1)

            iteration(0, FIRST)
            with pe.Fori(1, NB) as it:
                iteration(it, BOTH)
            iteration(NB, LAST)

        @block.scalar
        def _(act):
            act.wait_ge(const_in, 16 * 11)

            def fn(dst, src, func, **kw):
                return nc.scalar.activation(dst, src, func, **kw)

            def iteration(it, f):
                for step in STEPS[f]:
                    kind = step[0]
                    g = INDEX[f].get(step)
                    if kind == "EXP":
                        n = step[1]
                        act.wait_ge(max_done.sem, max_done.value(it, n + 1))
                        fn(exp_bias[:, n % 4:n % 4 + 1], neg_max[:, n % 4:n % 4 + 1], ACT.Copy, scale=CH ** -0.5)\
                            .then_inc(bias_done.sem, 1)
                        act.wait_ge(bias_done.sem, bias_done.value(it, n + 1))
                        if n >= 2:
                            act.wait_ge(pt_full.sem, pt_full.value(it, n - 1))
                        fn(probs[n % 2][:], scores[n % 2][:], ACT.Exp, bias=exp_bias[:, n % 4:n % 4 + 1],
                           scale=CH ** -0.5, accum_out=row_sum[:, n % 16:n % 16 + 1]).then_inc(exp_done.sem, 1)
                    elif kind == "T":
                        n = step[1]
                        act.wait_ge(pt_full.sem, pt_full.value(it, n + 1))
                        fn(pt[:, n % 2, :, n // 2 % 2 * P:(n // 2 % 2 + 1) * P], pt_ps[:], ACT.Copy)\
                            .then_inc(pt_copied.sem, 1)
                    elif kind == "AV":
                        c = step[1]
                        act.wait_ge(inv_done.sem, inv_done.value(it, c + 1))
                        fn(inv_wide[:], inv_sum[:, c % 2, :].unsqueeze(2).broadcast_to((P, 4, CH)), ACT.Copy)\
                            .then_inc(wide_done.sem, 1)
                        act.wait_ge(product.sem, products(f, it, step))
                        if c > 0:
                            for which, count in copies(f, it, ("AV", c - 1)):
                                act.wait_ge(emptied[which].sem, count)
                        fn(inv_q[:], bank[g % 2][:, 2 * P:4 * P], ACT.Copy).then_inc(inv_q_done.sem, 1)
                    elif kind == "V":
                        act.wait_ge(product.sem, products(f, it, step))
                        tb = step[1]
                        fn(vy[:, 1:PAIRS + 1, tb * P:(tb + 1) * P],
                           bank[g % 2][:].rearrange("p (j c) -> p j c", j=PAIRS), ACT.Copy)\
                            .then_inc(emptied[g % 2].sem, 1)
                    elif kind == "QK":
                        _, j, t, h = step
                        act.wait_ge(product.sem, products(f, it, step))
                        cols = slice(h * HALF, (h + 1) * HALF)
                        for hd in range(2):
                            src = bank[g % 2][hd * CH:(hd + 1) * CH, :]
                            bias = qkb_sb[hd * CH:(hd + 1) * CH, 2 * j + hd, t:t + 1]
                            if t == 0:
                                last = fn(q_st[0:CH, hd, cols], src, ACT.Identity, bias=bias)
                            else:
                                fn(k_st[CH:P, hd, 0, cols], src, ACT.Identity, bias=bias)
                                last = fn(k_st[0:CH, hd, 0, cols], src, ACT.Identity, bias=bias)
                        last.then_inc(high_done.sem, 1)
                        if t == 1:
                            for which, count in copies(f, it, step):
                                act.wait_ge(emptied[which].sem, count)
                            for hd in range(2):
                                last = fn(k_st[CH:P, hd, 1, cols], k_st[0:CH, hd, 1, cols].bitcast(F32), ACT.Copy)
                            last.then_inc(twice_done.sem, 1)
                    elif kind == "P1":
                        _, m, h = step
                        t = m % 3
                        act.wait_ge(product.sem, products(f, it, step))
                        if m >= 3:
                            act.wait_ge(conv_step.sem, conv_step.value(it, (m - 2) * CONV_STEPS))
                        rows = slice(PAD + h * H // 2, PAD + (h + 1) * H // 2)
                        src = bank[g % 2][:]
                        fn(pads[m % 3][:, rows, PAD:PAD + W], src.rearrange("p (a b) -> p a b", b=W), ACT.Copy)
                        dst = q_orig if t == 0 else kv_raw
                        fn(dst[:, h * HALF:(h + 1) * HALF], src, ACT.Copy if t == 2 else ACT.Relu)\
                            .then_inc(emptied[g % 2].sem, 1)
                    elif kind in ("PW", "TK", "TV", "TB"):
                        act.wait_ge(product.sem, products(f, it, step))
                        src = bank[g % 2][:]
                        h = step[-1]
                        cols = slice(h * HALF, (h + 1) * HALF)
                        src3 = src.rearrange("p (a b) -> p a b", b=P)
                        what = step[1] % 3 if kind == "PW" else {"TK": 1, "TV": 2, "TB": 3}[kind]
                        if what == 0:
                            last = fn(q_agg[:, cols], src, ACT.Relu)
                        elif what == 1:
                            last = fn(k_t[:, 4 * h:4 * h + 4, :], src3, ACT.Relu)
                        elif what == 2:
                            last = fn(v_t[:, 4 * h:4 * h + 4, 0:P], src3, ACT.Copy)
                        else:
                            last = fn(feat[:, SETS * step[1] + step[2], cols], src, ACT.Copy)
                        last.then_inc(emptied[g % 2].sem, 1)
                    elif kind == "PROJ":
                        i = step[1]
                        ob, h = divmod(i, 2)
                        for which, count in copies(f, it, step):
                            act.wait_ge(emptied[which].sem, count)
                        dst = out[bass.ds(it - 1, 1)] if not isinstance(it, int) else out[it - 1:it]
                        dst = dst[:, ob * P:(ob + 1) * P, h * HALF:(h + 1) * HALF]
                        act.dma_start(dst.rearrange("a p t -> (a p) t"), y_out[i % 2]).then_inc(out_sent[i % 2].sem, 16)
                        if i == 2 * CB - 1:
                            for s in out_sent:
                                act.wait_ge(s.sem, s.value(it, CB))

            iteration(0, FIRST)
            with act.Fori(1, NB) as it:
                iteration(it, BOTH)
            iteration(NB, LAST)

        @block.gpsimd
        def _(pool):
            pool.wait_ge(setup_dve, 1)
            with pool.Fori(0, NB) as it:
                pool.wait_ge(var_done.sem, it + 1)
                nc.gpsimd.tensor_tensor(gn[:, 3:4], gn[:, 4:5], gn[:, 5:6], ALU.pow).then_inc(std_done.sem, 1)

        @block.vector
        def _(dve):
            v = nc.vector
            for p in pads:
                v.memset(p[:], 0.0)
            v.memset(gn[:, 5:6], -0.5)
            v.memset(v_t[:, :, P:P + 1], 1.0).then_inc(setup_dve, 1)
            dve.wait_ge(const_in, 16 * 11)
            for m in range(BLOCKS):
                last = v.tensor_tensor(pw_bd[:, m, :].rearrange("p (h c) -> p h c", c=DIM),
                                       pw_dense[:, m, :].unsqueeze(1).broadcast_to((P, HEADS_SET, DIM)),
                                       bdmask[:].rearrange("p (h c) -> p h c", c=DIM), ALU.mult)
            last.then_inc(setup_dve, 1)
            dve.wait_ge(setup_pe, 1)
            v.tensor_tensor(outb2[:], scores[0][:, 0:CB], outb_sb[:], ALU.add).then_inc(setup_dve, 1)
            dve.wait_ge(setup_dve, 3)

            def iteration(it, f):
                links = [0]

                def link(ins):
                    links[0] += 1
                    ins.then_inc(link_done.sem, 1)
                    dve.wait_ge(link_done.sem, link_done.value(it, links[0]))

                for step in STEPS[f]:
                    kind = step[0]
                    g = INDEX[f].get(step)
                    if kind == "MAX":
                        n = step[1]
                        dve.wait_ge(scores_full.sem, scores_full.value(it, n + 1))
                        v.tensor_reduce(neg_max[:, n % 4:n % 4 + 1], scores[n % 2][:], AX_X, ALU.max, negate=True)\
                            .then_inc(max_done.sem, 1)
                    elif kind == "CONV":
                        _, m, i = step
                        if i == 0:
                            for which, count in copies(f, it, ("P1", m, 0), ("P1", m, 1)):
                                dve.wait_ge(emptied[which].sem, count)
                        full = acc[m % 2]
                        at = m * CONV_STEPS + i
                        if i == TAP_STEPS:
                            dve.wait_ge(conv_step.sem, conv_step.value(it, at))
                            v.tensor_tensor(full[:], full[:], side[:], ALU.add).then_inc(conv_step.sem, 1)
                            continue
                        dst = (full, side)[CHAIN[i]]
                        ty, tx = divmod(i, TAPS)
                        src = pads[m % 3][:, ty:ty + H, tx:tx + W]
                        wt = dw_sb[:, m, i:i + 1]
                        before = [k for k in range(i) if CHAIN[k] == CHAIN[i]]
                        if before:
                            dve.wait_ge(conv_step.sem, conv_step.value(it, m * CONV_STEPS + before[-1] + 1))
                            v.scalar_tensor_tensor(dst[:], src, wt, dst[:], ALU.mult, ALU.add)\
                                .then_inc(conv_step.sem, 1)
                        else:
                            if CHAIN[i] == 1:
                                if m > 0:
                                    dve.wait_ge(conv_step.sem, conv_step.value(it, m * CONV_STEPS))
                            elif m >= 2:
                                dve.wait_ge(product.sem, products(f, it, ("PW", m - 2, 1)))
                            v.tensor_scalar(dst[:], src, wt, None, ALU.mult).then_inc(conv_step.sem, 1)
                    elif kind == "STATS":
                        dve.wait_ge(x_in.sem, x_in.value(it, 1))
                        for i in range(2 * CB):
                            last = v.bn_stats(bn6[:, i, :], u[:, i // 2, i % 2 * HALF:(i % 2 + 1) * HALF])
                        link(last)
                        v.tensor_copy(gn[:, 6:7], gn[:, 5:6])
                        v.bn_aggr(mv[:], bn6[:].rearrange("p a b -> p (a b)")).then_inc(stats_done.sem, 1)
                    elif kind == "MEAN":
                        dve.wait_ge(product.sem, products(f, it, step))
                        ps = bank[g % 2][:, 0:1]
                        link(v.tensor_tensor(gn[:, 0:1], mv[:, 0:1], ps, ALU.subtract))
                        v.tensor_copy(gn[:, 2:3], ps).then_inc(emptied[g % 2].sem, 1)
                        v.tensor_scalar(gn[:, 1:2], gn[:, 0:1], gn[:, 0:1], mv[:, 1:2], ALU.mult, ALU.add)\
                            .then_inc(stats_done.sem, 1)
                    elif kind == "VAR":
                        dve.wait_ge(product.sem, products(f, it, step))
                        for which, count in copies(f, it, ("MEAN",)):
                            dve.wait_ge(emptied[which].sem, count)
                        v.tensor_scalar(gn[:, 4:5], bank[g % 2][:, 0:1], GN_EPS, None, ALU.add)\
                            .then_inc(var_done.sem, 1)
                        dve.wait_ge(std_done.sem, std_done.value(it, 1))
                        link(v.tensor_scalar(gn_a[:], gnw_sb[:], gn[:, 3:4], None, ALU.mult))
                        link(v.scalar_tensor_tensor(gn_nb[:], gn_a[:], gn[:, 2:3], gnb_sb[:], ALU.mult, ALU.subtract))
                        for k in range(CB):
                            if k < CB - 1:
                                v.tensor_scalar(u[:, k, :], u[:, k, :], gn_a[:, k:k + 1], gn_nb[:, k:k + 1],
                                                ALU.mult, ALU.subtract)
                            else:
                                link(v.tensor_scalar(u[:, k, :], u[:, k, :], gn_a[:, k:k + 1], gn_nb[:, k:k + 1],
                                                     ALU.mult, ALU.subtract))
                        v.tensor_copy(gn[:, 0:1], bank[g % 2][:, 0:1]).then_inc(emptied[g % 2].sem, 1)
                        v.tensor_copy(mv[:, 0:1], gn_a[:, 0:1]).then_inc(u_ready.sem, 1)
                    elif kind == "QK":
                        _, j, t, h = step
                        dve.wait_ge(high_done.sem, high_done.value(it, 4 * j + 2 * t + h + 1))
                        cols = slice(h * HALF, (h + 1) * HALF)
                        for hd in range(2):
                            high = (q_st[0:CH, hd, cols] if t == 0 else k_st[0:CH, hd, 0, cols]).bitcast(F32)
                            dst = q_st[CH:P, hd, cols] if t == 0 else k_st[0:CH, hd, 1, cols]
                            last = v.scalar_tensor_tensor(dst, bank[g % 2][hd * CH:(hd + 1) * CH, :],
                                                          qkb_sb[0:CH, 2 * j + hd, t:t + 1], high,
                                                          ALU.add, ALU.subtract)
                        last.then_inc(emptied[g % 2].sem, 1)
                    elif kind == "RECIP":
                        c = step[1]
                        dve.wait_ge(exp_done.sem, exp_done.value(it, 4 * c + 4))
                        v.reciprocal(inv_sum[:, c % 2, :], row_sum[:, 4 * c % 16:4 * c % 16 + 4])\
                            .then_inc(inv_done.sem, 1)
                    elif kind == "AV":
                        c = step[1]
                        dve.wait_ge(inv_q_done.sem, inv_q_done.value(it, c + 1))
                        v.tensor_tensor(vy[:, c // 4, c % 4 * 2 * P:(c % 4 + 1) * 2 * P], bank[g % 2][:, 0:2 * P],
                                        inv_q[:], ALU.mult).then_inc(emptied[g % 2].sem, 1)
                    elif kind == "VK":
                        dve.wait_ge(product.sem, products(f, it, step))
                        ps = bank[g % 2]
                        v.tensor_tensor(vk[:, 0:P], ps[:, 0:P], bdmask[:], ALU.mult)
                        v.tensor_scalar(vk[:, P:NW], hmask[:], ps[:, P:P + 1], None, ALU.mult)\
                            .then_inc(emptied[g % 2].sem, 1)
                    elif kind == "NUM":
                        _, s, j, g3 = step
                        dve.wait_ge(product.sem, products(f, it, step))
                        nb = min(QB, 3 * g3 + 3) - 3 * g3
                        ps = bank[g % 2][:, 0:nb * NW].rearrange("p (a b) -> p a b", b=NW)
                        d = [den[:, g % 2, i, 0:nb * HEADS_SET].rearrange("p (a b) -> p a b", b=HEADS_SET)
                             for i in range(2)]
                        link(v.tensor_scalar(d[0], ps[:, :, P:NW], ATT_EPS, None, ALU.add))
                        link(v.reciprocal(d[1], d[0]))
                        v.tensor_tensor(num_t[:, 3 * g3:3 * g3 + nb, :].rearrange("p a (h c) -> p a h c", c=DIM),
                                        ps[:, :, 0:P].rearrange("p a (h c) -> p a h c", c=DIM),
                                        d[1].unsqueeze(3).broadcast_to((P, nb, HEADS_SET, DIM)), ALU.mult)\
                            .then_inc(emptied[g % 2].sem, 1)
                    elif kind == "PROJ":
                        i = step[1]
                        ob, h = divmod(i, 2)
                        dve.wait_ge(product.sem, products(f, it, step))
                        if i >= 2:
                            dve.wait_ge(out_sent[i % 2].sem, out_sent[i % 2].value(it, i // 2))
                        v.tensor_tensor(y_out[i % 2], bank[g % 2][:], x1[:, ob, h * HALF:(h + 1) * HALF], ALU.add)\
                            .then_inc(emptied[g % 2].sem, 1)
                    elif kind == "OUT":
                        i = step[1]
                        ob, h = divmod(i, 2)
                        dve.wait_ge(product.sem, products(f, it, step))
                        dve.wait_ge(x_res_in[i % 2].sem, x_res_in[i % 2].value(it, i // 2 + 1))
                        v.scalar_tensor_tensor(x1[:, ob, h * HALF:(h + 1) * HALF], bank[g % 2][:], outb2[:, ob:ob + 1],
                                               x_res[i % 2], ALU.add, ALU.add).then_inc(emptied[g % 2].sem, 1)
                assert links[0] == (LINKS0 if f[0] else 0) + (LINKS1 if f[1] else 0), links

            iteration(0, FIRST)
            with dve.Fori(1, NB) as it:
                iteration(it, BOTH)
            iteration(NB, LAST)


def kernel(x, L0_conv_gn_weight, L0_conv_gn_bias, L0_conv_qkv_w, L0_conv_qkv_b, L0_conv_out_w, L0_conv_out_b,
           L1_conv_w_qkv, L1_conv_w_dw, L1_conv_w_pw, L1_conv_w_proj):
    import concourse.bacc as bacc
    from concourse.bass_utils import run_bass_kernel_spmd

    def lay(a):
        return np.ascontiguousarray(a)

    def per_block(a):
        return lay(np.asarray(a).reshape(-1, P).T)

    x, qkv_w, qkv_b = np.asarray(x), np.asarray(L0_conv_qkv_w), np.asarray(L0_conv_qkv_b)
    w_t = qkv_w.T.reshape(CB, P, 3, PAIRS, P)
    order = np.arange(3 * C).reshape(SETS, HEADS_SET, 3, DIM).transpose(0, 2, 1, 3).reshape(-1)
    w1 = np.asarray(L1_conv_w_qkv).reshape(3 * C, C)[order].reshape(SETS, 3, P, CB, P)
    bias = qkv_b[:2 * C].reshape(2, NHEAD, CH).transpose(2, 1, 0)
    arrays = {
        "x": lay(x.reshape(NB, C, L)),
        "w0qk": lay(w_t[:, :, 0:2].transpose(3, 1, 0, 2, 4)),
        "w0v": lay(w_t[:, :, 2].reshape(CB, P, C).transpose(1, 0, 2)),
        "w0out": lay(np.asarray(L0_conv_out_w).T.reshape(CB, P, C).transpose(1, 0, 2)),
        "w1": lay(w1.transpose(0, 4, 3, 1, 2)),
        "wproj": lay(np.asarray(L1_conv_w_proj).reshape(C, 2 * C).T.reshape(2 * SETS, P, C).transpose(1, 0, 2)),
        "pw": lay(np.asarray(L1_conv_w_pw).reshape(3 * C, DIM)[order].reshape(BLOCKS, HEADS_SET, DIM, DIM)
                  .transpose(1, 3, 0, 2).reshape(P, BLOCKS, DIM)),
        "dw": lay(np.asarray(L1_conv_w_dw).reshape(3 * C, TAPS * TAPS)[order].reshape(BLOCKS, P, -1)
                  .transpose(1, 0, 2)),
        "gnw": per_block(L0_conv_gn_weight),
        "gnb": per_block(L0_conv_gn_bias),
        "qk_bias": lay(np.concatenate([bias, bias], 0)),
        "v_bias": per_block(qkv_b[2 * C:]),
        "out_bias": per_block(L0_conv_out_b),
        "identity": np.eye(P, dtype=np.float32),
        "block_mask": np.kron(np.eye(HEADS_SET), np.ones((DIM, DIM))).astype(np.float32),
        "head_mask": np.kron(np.eye(HEADS_SET), np.ones((DIM, 1))).astype(np.float32),
        "ones": np.full((P, P), 1.0 / P, np.float32),
    }
    nc = bacc.Bacc("TRN2", target_bir_lowering=False, num_devices=1, dynamic_dma_scratch_size=1024)
    args = {n: nc.dram_tensor(f"in_{n}", a.shape, F32, kind="ExternalInput").ap() for n, a in arrays.items()}
    out = nc.dram_tensor("out_0", (NB, C, L), F32, kind="ExternalOutput").ap()
    build(nc, out=out, **args)
    r = run_bass_kernel_spmd(nc, [{f"in_{n}": a for n, a in arrays.items()}], core_ids=[0])
    return r.results[0]["out_0"].reshape(NB, C, H, W)
```

```python
from contextlib import ExitStack

import numpy as np
import concourse.bass as bass
from concourse import mybir

P = 128
F32 = mybir.dt.float32
F32R = mybir.dt.float32r
ALU = mybir.AluOpType
ACT = mybir.ActivationFunctionType
AX_X = mybir.AxisListType.X

NB, C, H, W = 8, 512, 32, 32
L = H * W
CB = C // P
NHEAD, CH = 8, 64
PAIRS = NHEAD // 2
QB = L // P
GN_EPS = 1e-5
TAPS = 5
PAD = TAPS // 2
HP = H + 2 * PAD
DIM = 8
HEADS_SET = P // DIM
SETS = C // P
BLOCKS = 3 * SETS
ATT_EPS = 1e-15
HALF = 512
UNITS = NHEAD * QB
NW = P + HEADS_SET

FILL_FIRST, FILL_LAST = 20, 5
QK_AT = (6, 8, 10, 12)
RING = 4

TAP_STEPS = TAPS * TAPS
CONV_STEPS = TAP_STEPS + 1
CHAIN = [1 if i < 3 else (0 if i % 2 else 1) for i in range(TAP_STEPS)]
CHUNK = [6, 5, 5, 5, 5]


def layer1_chunks():
    chunks = []
    for m in range(BLOCKS + 1):
        j, t = divmod(m, 3)
        window = [[] for _ in CHUNK]
        if t != 2 and m < BLOCKS:
            window[1].append(("P1", m + 1, 0))
            window[3].append(("P1", m + 1, 1))
        if t == 1:
            window[0] += [("PW", m - 1, 0), ("PW", m - 1, 1), ("TK", j, 0)]
            window[1] += [("TK", j, 1)]
            if m > 1:
                window[2] += [("TB", 1, j - 1, h) for h in range(2)]
            window[4] += [("TV", j, 0), ("TV", j, 1)]
        if t == 2:
            window[0] += [("VK", 0, j)]
            window[1] += [("NUM", 0, j, 0), ("NUM", 0, j, 1)]
            window[2] += [("NUM", 0, j, 2), ("PW", m - 1, 0)]
            window[3] += [("PW", m - 1, 1)]
            if m + 1 < BLOCKS:
                window[2].insert(1, ("P1", m + 1, 0))
                window[3].insert(0, ("P1", m + 1, 1))
            window[4] += [("TB", 0, j, h) for h in range(2)]
        if t == 0 and m > 0:
            last = m == BLOCKS
            window[0] += [("PW", m - 1, 0), ("PW", m - 1, 1)]
            window[2] += [("VK", 1, j - 1)]
            window[3] += [("NUM", 1, j - 1, 0)]
            window[4] += [("NUM", 1, j - 1, 1), ("NUM", 1, j - 1, 2)]
            if last:
                window[4] += [("TB", 1, j - 1, h) for h in range(2)]
        for r, groups in enumerate(window):
            lo = sum(CHUNK[:r])
            steps = [("CONV", m, i) for i in range(lo, lo + CHUNK[r])] if m < BLOCKS else []
            if groups or steps:
                chunks.append((groups, steps))
    return chunks


GROUPS = ("P1", "MEAN", "VAR", "V", "QK", "PW", "TK", "TV", "VK", "NUM", "TB", "AV", "SPREAD", "PROJ", "OUT")
BY_VECTOR = ("VK", "NUM", "PROJ", "OUT")


def timeline(l0, l1, l2):
    chunks = layer1_chunks() if l1 else []
    done, out = [0], []

    def add(groups, steps):
        steps, late = list(steps), []
        per = -(-len(steps) // max(1, len(groups)))
        for g in groups:
            out.append(g)
            part, steps = steps[:per], steps[per:]
            out.extend(part[:1])
            out.extend(late)
            late = [("COPY", g)] if g[0] in BY_VECTOR else []
            out.extend(part[1:])
        out.extend(steps[:1] + late + steps[1:])

    def take(upto):
        groups, steps = [], []
        while done[0] < min(upto, len(chunks)):
            groups += chunks[done[0]][0]
            steps += chunks[done[0]][1]
            done[0] += 1
        return groups, steps

    if l1:
        out += [("P1", 0, 0), ("P1", 0, 1)]
    if l0:
        out.append(("STATS",))
    first = [("PROJ", i) for i in range(2 * CB)] if l2 else []
    if l0:
        first.insert(min(1, len(first)), ("MEAN",))
        first.insert(min(3, len(first)), ("VAR",))
        first += [("V", i) for i in range(QB)] + [("QK", 0, t, h) for t in (1, 0) for h in range(2)]
    fill = FILL_FIRST if l0 else 13
    for i, step in enumerate(first):
        g, s = take((i + 1) * fill // len(first))
        add([step] + g, s)
    if l0:
        out += [("SPLIT", 0), ("S", 0), ("MAX", 0), ("EXP", 0)]
        rest = len(chunks) - done[0] - FILL_LAST
        begun = done[0]
        span = 2 * QB
        for n in range(UNITS):
            g, s = take(begun + (n + 1) * rest // UNITS if l1 else 0)
            nxt = n + 1 < UNITS
            j, at = divmod(n, span)
            if j + 1 < PAIRS and at in QK_AT:
                r = QK_AT.index(at)
                g = [("QK", j + 1, 1 - r // 2, r % 2)] + g
            c = n // 4
            scaling = [[("RECIP", c - 1)], [("WIDE", c - 1)], [("SPREAD", c - 1)], [("NORM", c - 1)]][n % 4] if c else []
            k = len(s) // 2
            if nxt and at == span - 1:
                out += [("T", n), ("SPLIT", j + 1), ("AV", c)]
                add(g, s[:k])
                out += [("S", n + 1), ("MAX", n + 1)] + scaling + [("EXP", n + 1)] + s[k:]
                continue
            if nxt:
                out.append(("S", n + 1))
            add(g[:len(g) // 2], s[:k])
            if nxt:
                out.append(("MAX", n + 1))
            add(g[len(g) // 2:], s[k:-1])
            out += scaling
            if n % 4 == 0 and at > 0:
                out.append(("AV", c - 1))
            if nxt:
                out.append(("EXP", n + 1))
            out += s[-1:] if k or s else []
            out.append(("T", n))
        c = UNITS // 4 - 1
        out += [("AV", c), ("RECIP", c), ("WIDE", c)]
        for i in range(2 * CB):
            if i == CB - 2:
                out += [("SPREAD", c), ("NORM", c)]
            g, s = take(done[0] + 1 if i % 2 else 0)
            add([("OUT", i)] + g, s)
    while done[0] < len(chunks):
        g, s = take(done[0] + 1)
        add(g, s)
    return out


def build(nc, x, w0qk, w0v, w0out, w1, wproj, pw, dw, gnw, gnb, qk_bias, v_bias, out_bias,
          identity, block_mask, head_mask, ones, out):
    FLAGS = [(True, False, False), (True, True, False), (True, True, True), (False, True, True), (False, False, True)]
    BEGIN, SECOND, STEADY, DRAIN, END = FLAGS
    STEPS = {f: timeline(*f) for f in FLAGS}
    INDEX = {}
    for f, steps in STEPS.items():
        INDEX[f] = {s: i for i, s in enumerate([s for s in steps if s[0] in GROUPS])}
    G0, G2 = len(INDEX[BEGIN]), len(INDEX[END])
    G1 = len(INDEX[SECOND]) - G0
    assert len(INDEX[STEADY]) == G0 + G1 + G2 and G0 % 2 == 0 and G1 % 2 == 0 and G2 % 2 == 0

    x1_dram = nc.dram_tensor("x1_dram", (NB, C, L), F32, kind="Internal").ap()
    ctx = ExitStack()
    with ctx:
        def sb(name, shape, dt=F32):
            return ctx.enter_context(nc.sbuf_tensor(name, shape, dt))

        def psum(name, shape):
            return ctx.enter_context(nc.psum_tensor(name, shape, F32))

        def sem(name):
            return ctx.enter_context(nc.semaphore(name))

        class Signal:

            def __init__(self, name, l0, l1, l2=0, by=1):
                self.sem, self.l0, self.l1, self.l2, self.by = sem(name), l0, l1, l2, by

            def value(self, it, n):
                if isinstance(it, int):
                    k = self.l0 * min(it, NB) + self.l1 * min(max(it - 1, 0), NB) + self.l2 * max(it - 2, 0)
                    return (k + n) * self.by
                return it * ((self.l0 + self.l1 + self.l2) * self.by) + (n - self.l1 - 2 * self.l2) * self.by

        def positive(v):
            return not (isinstance(v, int) and v <= 0)

        w_small = sb("w_small", [P, CB, C])
        w0qk_sb = sb("w0qk_sb", [P, CB, 2, P])
        w1_sb = sb("w1_sb", [P, CB, 3, P])
        pw_dense = sb("pw_dense", [P, BLOCKS, DIM])
        pw_bd = sb("pw_bd", [P, BLOCKS, P])
        dw_sb = sb("dw_sb", [P, BLOCKS, TAPS * TAPS])
        gnw_sb = sb("gnw_sb", [P, CB])
        gnb_sb = sb("gnb_sb", [P, CB])
        qkb_sb = sb("qkb_sb", [P, PAIRS, 2])
        vb_sb = sb("vb_sb", [P, PAIRS])
        outb_sb = sb("outb_sb", [P, CB])
        outb2 = sb("outb2", [P, CB])
        ident = sb("ident", [P, P])
        bdmask = sb("bdmask", [P, P])
        hmask = sb("hmask", [P, HEADS_SET])
        mean_w = sb("mean_w", [P, P])
        u = sb("u", [P, CB, L])
        qk_raw = sb("qk_raw", [P, 2, L])
        q_st = sb("q_st", [P, 2, L], F32R)
        k_st = sb("k_st", [P, 2, 2, L], F32R)
        vy = sb("vy", [P, PAIRS + 1, L])
        probs = [sb(f"probs{i}", [P, L]) for i in range(2)]
        pt = sb("pt", [P, 2, QB, 2 * P])
        x1 = sb("x1", [P, CB, L])
        pads = [sb(f"pad{i}", [P, HP, HP]) for i in range(3)]
        acc = [sb(f"acc{i}", [P, H, W]) for i in range(2)]
        side = sb("side", [P, H, W])
        q_orig = sb("q_orig", [P, L])
        q_agg = sb("q_agg", [P, L])
        kv_raw = sb("kv_raw", [P, L])
        k_t = sb("k_t", [P, QB, P])
        v_t = sb("v_t", [P, QB, P + 1])
        vk = sb("vk", [P, NW])
        den = sb("den", [P, 2, 2, 3 * HEADS_SET])
        num_t = sb("num_t", [P, QB, P])
        feat = sb("feat", [P, 2 * SETS, L])
        row_sum = sb("row_sum", [P, 16])
        inv_sum = sb("inv_sum", [P, 2, 4])
        inv_wide = sb("inv_wide", [P, 4, CH])
        inv_q = sb("inv_q", [P, 2 * P])
        neg_max = sb("neg_max", [P, 4])
        exp_bias = sb("exp_bias", [P, 4])
        bn6 = sb("bn6", [P, 2 * CB, 6])
        mv = sb("mv", [P, 2])
        gn = sb("gn", [P, 7])
        gn_a = sb("gn_a", [P, CB])
        gn_nb = sb("gn_nb", [P, CB])
        wproj_sb = pt[:, :, :, :].rearrange("p a b c -> p (a b c)").rearrange("p (b n) -> p b n", b=2 * SETS)
        part = [probs[i // 2][:, i % 2 * HALF:(i % 2 + 1) * HALF] for i in range(RING)]

        scores = [psum(f"scores{i}", [P, L]) for i in range(2)]
        pt_ps = psum("pt_ps", [P, QB, P])
        bank = [psum(f"bank{i}", [P, HALF]) for i in range(2)]

        const_in = sem("const_in")
        w0out_pre = sem("w0out_pre")
        setup_dve = sem("setup_dve")
        setup_pe = sem("setup_pe")
        x_in = Signal("x_in", 1, 0, 0, 16)
        w0v_in = Signal("w0v_in", 1, 0, 0, 16)
        w0qk_in = Signal("w0qk_in", PAIRS, 0, 0, 16)
        w0out_in = Signal("w0out_in", 1, 0, 0, 16)
        w1_in = Signal("w1_in", 0, SETS, 0, 16)
        wproj_in = Signal("wproj_in", 0, 1, 0, 16)
        res_in = [Signal(f"res_in{i}", 0, 0, 2 * CB // RING, 16) for i in range(RING)]
        x_again_in = Signal("x_again_in", 1, 0, 0, 16)
        x1_sent = Signal("x1_sent", 1, 0, 0, 16)
        out_sent = [Signal(f"out_sent{i}", 0, 0, 2 * CB // RING, 16) for i in range(RING)]
        product = Signal("product", G0, G1, G2)
        emptied = [Signal(f"emptied{i}", G0 // 2, G1 // 2, G2 // 2) for i in range(2)]
        scores_full = Signal("scores_full", UNITS, 0)
        max_done = Signal("max_done", UNITS, 0)
        bias_done = Signal("bias_done", UNITS, 0)
        exp_done = Signal("exp_done", UNITS, 0)
        pt_full = Signal("pt_full", UNITS, 0)
        pt_copied = Signal("pt_copied", UNITS, 0)
        inv_done = Signal("inv_done", UNITS // 4, 0)
        wide_done = Signal("wide_done", UNITS // 4, 0)
        norm_done = Signal("norm_done", UNITS // 4, 0)
        high_done = Signal("high_done", 2 * PAIRS, 0)
        low_done = Signal("low_done", 2 * PAIRS, 0)
        twice_done = Signal("twice_done", 2 * PAIRS, 0)
        affine_done = Signal("affine_done", 1, 0)
        stats_done = Signal("stats_done", 2, 0)
        var_done = Signal("var_done", 1, 0)
        std_done = Signal("std_done", 1, 0)
        u_ready = Signal("u_ready", 1, 0)
        conv_step = Signal("conv_step", 0, BLOCKS * CONV_STEPS)
        LINKS0, LINKS1 = 4, 2 * SETS * 3 * 2
        link_done = Signal("link_done", LINKS0, LINKS1)

        def products(f, it, step):
            return product.value(it, INDEX[f][step] + 1)

        def copies(f, it, *steps):
            last = {}
            for g in sorted(INDEX[f][s] for s in steps):
                last[g % 2] = g
            return [(b, emptied[b].value(it, g // 2 + 1)) for b, g in last.items()]

        block = ctx.enter_context(nc.Block())

        @block.sync
        def _(sp):
            for dst, src in ((pw_dense, pw), (dw_sb, dw), (gnw_sb, gnw), (gnb_sb, gnb), (qkb_sb, qk_bias),
                             (vb_sb, v_bias), (outb_sb, out_bias), (ident, identity), (bdmask, block_mask),
                             (hmask, head_mask), (mean_w, ones)):
                sp.dma_start(dst[:], src).then_inc(const_in, 16)

            def load_x(it):
                src = x[bass.ds(it, 1)] if not isinstance(it, int) else x[it:it + 1]
                sp.dma_start(u[:], src.rearrange("a (k p) t -> p (a k) t", p=P)).then_inc(x_in.sem, 16)

            def load_x_again(it):
                src = x[bass.ds(it, 1)] if not isinstance(it, int) else x[it:it + 1]
                sp.dma_start(x1[:], src.rearrange("a (k p) t -> p (a k) t", p=P)).then_inc(x_again_in.sem, 16)

            def load_w0qk(j):
                sp.dma_start(w0qk_sb[:], w0qk[j]).then_inc(w0qk_in.sem, 16)

            def load_w1(j):
                sp.dma_start(w1_sb[:], w1[j]).then_inc(w1_in.sem, 16)

            load_x(0)
            sp.dma_start(w_small[:], w0v).then_inc(w0v_in.sem, 16)
            load_w0qk(0)
            load_w1(0)
            sp.dma_start(wproj_sb[:, 0:CB, :], w0out).then_inc(w0out_pre, 16)

            def image(t, i):
                return t[i:i + 1] if isinstance(i, int) else t[bass.ds(i, 1)]

            def iteration(it, f, more):
                l0, l1, l2 = f
                last_image = it - 2 if isinstance(it, int) else sp.snap(it - 2)
                if l2:
                    if f == END:
                        sp.wait_ge(x1_sent.sem, x1_sent.value(it - 1, 0))
                    else:
                        sp.wait_ge(pt_full.sem, pt_full.value(it, 0))
                    for i in range(2 * CB):
                        if i >= RING or f == END:
                            sp.wait_ge(out_sent[i % RING].sem, out_sent[i % RING].value(it, i // RING))
                        ob, h = divmod(i, 2)
                        src = image(x1_dram, last_image)[:, ob * P:(ob + 1) * P, h * HALF:(h + 1) * HALF]
                        sp.dma_start(part[i % RING], src.rearrange("a p t -> (a p) t")).then_inc(res_in[i % RING].sem, 16)
                loads = []
                if l0:
                    loads.append((("V", QB - 1), "w0out", 0))
                    loads += [(("QK", j, 0, 1), "w0qk", j + 1) for j in range(PAIRS) if j + 1 < PAIRS or more]
                    if l1:
                        loads.append((("P1", BLOCKS - 1, 1), "x", 0))
                    else:
                        load_x_again(it)
                if l1:
                    loads += [(("P1", 3 * j + 2, 1), "w1", j + 1) for j in range(SETS) if j + 1 < SETS or l0]
                for user, what, j in sorted(loads, key=lambda load: INDEX[f][load[0]]):
                    if what == "x":
                        for which, count in copies(f, it, user):
                            sp.wait_ge(emptied[which].sem, count)
                        load_x_again(it)
                        continue
                    sp.wait_ge(product.sem, products(f, it, user))
                    if what == "w0out":
                        sp.dma_start(w_small[:], w0out).then_inc(w0out_in.sem, 16)
                    elif what == "w1":
                        load_w1(j % SETS)
                    else:
                        load_w0qk(j % PAIRS)
                        if j == PAIRS:
                            load_x(it + 1)
                if l1:
                    if l0:
                        sp.wait_ge(product.sem, products(f, it, ("AV", UNITS // 4 - 1)))
                    elif l2:
                        sp.wait_ge(product.sem, products(f, it, ("PROJ", 2 * CB - 1)))
                    sp.dma_start(wproj_sb[:], wproj).then_inc(wproj_in.sem, 16)
                if l0:
                    if more:
                        for which, count in copies(f, it, ("OUT", 2 * CB - 1)):
                            sp.wait_ge(emptied[which].sem, count)
                        sp.dma_start(w_small[:], w0v).then_inc(w0v_in.sem, 16)

            iteration(0, BEGIN, True)
            iteration(1, SECOND, True)
            with sp.Fori(2, NB - 1) as it:
                iteration(it, STEADY, True)
            iteration(NB - 1, STEADY, False)
            iteration(NB, DRAIN, False)
            iteration(NB + 1, END, False)

        @block.tensor
        def _(pe):
            mm = nc.tensor.matmul
            pe.wait_ge(const_in, 16 * 11)
            pe.wait_ge(w0out_pre, 16)
            for ob in range(CB):
                for j in range(PAIRS):
                    last = mm(scores[0][:, ob:ob + 1], wproj_sb[:, j, ob * P:(ob + 1) * P], vb_sb[:, j:j + 1],
                              start=(j == 0), stop=(j == PAIRS - 1))
            last.then_inc(setup_pe, 1)
            pe.wait_ge(setup_dve, 3)

            def group(it, f, step):
                g = INDEX[f][step]
                b = bank[g % 2]
                if positive(emptied[g % 2].value(it, g // 2)):
                    pe.wait_ge(emptied[g % 2].sem, emptied[g % 2].value(it, g // 2))
                kind = step[0]
                if kind in ("MEAN", "VAR"):
                    pe.wait_ge(stats_done.sem, stats_done.value(it, 1 if kind == "MEAN" else 2))
                    rhs = mv[:, 0:1] if kind == "MEAN" else gn[:, 1:2]
                    last = mm(b[:, 0:1], mean_w[:], rhs, start=True, stop=True)
                elif kind == "V":
                    tb = step[1]
                    if tb == 0:
                        pe.wait_ge(u_ready.sem, u_ready.value(it, 1))
                        pe.wait_ge(w0v_in.sem, w0v_in.value(it, 1))
                    for k in range(CB):
                        last = mm(b[:], u[:, k, tb * P:(tb + 1) * P], w_small[:, k, :],
                                  start=(k == 0), stop=(k == CB - 1))
                elif kind == "QK":
                    _, j, t, h = step
                    if t == 1 and h == 0:
                        pe.wait_ge(w0qk_in.sem, w0qk_in.value(it, j + 1))
                    for k in range(CB):
                        last = mm(b[:], w0qk_sb[:, k, t, :], u[:, k, h * HALF:(h + 1) * HALF],
                                  start=(k == 0), stop=(k == CB - 1))
                elif kind == "AV":
                    c = step[1]
                    j = c // 4
                    pe.wait_ge(pt_copied.sem, pt_copied.value(it, 4 * c + 4))
                    if c == 0:
                        for which, count in copies(f, it, ("V", QB - 2), ("V", QB - 1)):
                            pe.wait_ge(emptied[which].sem, count)
                    for kb in range(QB):
                        for hd in range(2):
                            last = mm(b[hd * CH:(hd + 1) * CH, 0:2 * P],
                                      vy[:, j + 1, kb * P + hd * CH:kb * P + (hd + 1) * CH],
                                      pt[:, hd, kb, :], start=(kb == 0), stop=(kb == QB - 1))
                elif kind == "SPREAD":
                    c = step[1]
                    pe.wait_ge(wide_done.sem, wide_done.value(it, c + 1))
                    for q in range(2):
                        last = nc.tensor.transpose(b[:, q * P:(q + 1) * P],
                                                   inv_wide[:, 2 * q:2 * q + 2, :].rearrange("p a c -> p (a c)"),
                                                   ident[:])
                elif kind == "OUT":
                    h, ob = divmod(step[1], CB)
                    if step[1] == 0:
                        pe.wait_ge(w0out_in.sem, w0out_in.value(it, 1))
                    if ob == 0:
                        pe.wait_ge(norm_done.sem, norm_done.value(it, UNITS // 4 - 2 * (1 - h)))
                    for j in range(PAIRS):
                        last = mm(b[:], w_small[:, j, ob * P:(ob + 1) * P], vy[:, j, h * HALF:(h + 1) * HALF],
                                  start=(j == 0), stop=(j == PAIRS - 1))
                elif kind == "P1":
                    _, m, h = step
                    j, t = divmod(m, 3)
                    if h == 0 and t == 0:
                        pe.wait_ge(w1_in.sem, w1_in.value(it, j + 1))
                    if h == 0 and m == 0:
                        for i in range(2):
                            pe.wait_ge(emptied[i].sem, emptied[i].value(it, 0))
                    for k in range(CB):
                        last = mm(b[:], w1_sb[:, k, t, :], x1[:, k, h * HALF:(h + 1) * HALF],
                                  start=(k == 0), stop=(k == CB - 1))
                elif kind == "PW":
                    _, m, h = step
                    if h == 0:
                        pe.wait_ge(conv_step.sem, conv_step.value(it, (m + 1) * CONV_STEPS))
                    a = acc[m % 2][:].rearrange("p a b -> p (a b)")
                    if m % 3 == 0:
                        last = mm(b[:], pw_bd[:, m, :], a[:, h * HALF:(h + 1) * HALF], start=True, stop=True)
                    else:
                        for i in range(4):
                            tb = 4 * h + i
                            last = mm(b[:, i * P:(i + 1) * P], a[:, tb * P:(tb + 1) * P], pw_bd[:, m, :],
                                      start=True, stop=True)
                elif kind in ("TK", "TV"):
                    _, j, h = step
                    for which, count in copies(f, it, ("P1", 3 * j + (1 if kind == "TK" else 2), h)):
                        pe.wait_ge(emptied[which].sem, count)
                    for i in range(4):
                        tb = 4 * h + i
                        last = nc.tensor.transpose(b[:, i * P:(i + 1) * P], kv_raw[:, tb * P:(tb + 1) * P], ident[:])
                elif kind == "VK":
                    _, s, j = step
                    if s == 0:
                        for which, count in copies(f, it, *[(kind, j, h) for kind in ("TK", "TV") for h in range(2)]):
                            pe.wait_ge(emptied[which].sem, count)
                    else:
                        for which, count in copies(f, it, *[("PW", 3 * j + t, h) for t in (1, 2) for h in range(2)]):
                            pe.wait_ge(emptied[which].sem, count)
                    for tb in range(QB):
                        last = mm(b[:, 0:P + 1], k_t[:, tb, :], v_t[:, tb, :], start=(tb == 0), stop=(tb == QB - 1))
                elif kind == "NUM":
                    _, s, j, g3 = step
                    if g3 == 0:
                        for which, count in copies(f, it, ("VK", s, j), *[("P1" if s == 0 else "PW", 3 * j, h) for h in range(2)]):
                            pe.wait_ge(emptied[which].sem, count)
                    q = q_orig if s == 0 else q_agg
                    for i, tb in enumerate(range(3 * g3, min(QB, 3 * g3 + 3))):
                        last = mm(b[:, i * NW:(i + 1) * NW], q[:, tb * P:(tb + 1) * P], vk[:], start=True, stop=True)
                elif kind == "TB":
                    _, s, j, h = step
                    for which, count in copies(f, it, *[("NUM", s, j, g3) for g3 in ((0, 1) if h == 0 else (2,))]):
                        pe.wait_ge(emptied[which].sem, count)
                    for i in range(4):
                        last = nc.tensor.transpose(b[:, i * P:(i + 1) * P], num_t[:, 4 * h + i, :], ident[:])
                elif kind == "PROJ":
                    ob, h = divmod(step[1], 2)
                    if step[1] == 0:
                        pe.wait_ge(wproj_in.sem, wproj_in.value(it, 0))
                        if not f[1]:
                            for i in range(2):
                                pe.wait_ge(emptied[i].sem, emptied[i].value(it, 0))
                    for k in range(2 * SETS):
                        last = mm(b[:], wproj_sb[:, k, ob * P:(ob + 1) * P], feat[:, k, h * HALF:(h + 1) * HALF],
                                  start=(k == 0), stop=(k == 2 * SETS - 1))
                last.then_inc(product.sem, 1)

            def iteration(it, f):
                for step in STEPS[f]:
                    if step[0] in GROUPS:
                        group(it, f, step)
                    elif step[0] == "S":
                        n = step[1]
                        j, qb, hd = n // (2 * QB), n // 2 % QB, n % 2
                        if positive(exp_done.value(it, n - 1)):
                            pe.wait_ge(exp_done.sem, exp_done.value(it, n - 1))
                        if n % (2 * QB) < 2:
                            pe.wait_ge(twice_done.sem, twice_done.value(it, 2 * j + hd + 1))
                        for h in range(2):
                            for part in range(2):
                                last = mm(scores[hd][:, h * HALF:(h + 1) * HALF], q_st[:, hd, qb * P:(qb + 1) * P],
                                          k_st[:, hd, part, h * HALF:(h + 1) * HALF],
                                          start=(part == 0), stop=(part == 1))
                        last.then_inc(scores_full.sem, 1)
                    elif step[0] == "T":
                        n = step[1]
                        pe.wait_ge(exp_done.sem, exp_done.value(it, n + 1))
                        if positive(pt_copied.value(it, n)):
                            pe.wait_ge(pt_copied.sem, pt_copied.value(it, n))
                        for kb in range(QB):
                            last = nc.tensor.transpose(pt_ps[:, kb, :], probs[n % 2][:, kb * P:(kb + 1) * P], ident[:])
                        last.then_inc(pt_full.sem, 1)

            iteration(0, BEGIN)
            iteration(1, SECOND)
            with pe.Fori(2, NB) as it:
                iteration(it, STEADY)
            iteration(NB, DRAIN)
            iteration(NB + 1, END)

        @block.scalar
        def _(act):
            act.wait_ge(const_in, 16 * 11)

            def fn(dst, src, func, **kw):
                return nc.scalar.activation(dst, src, func, **kw)

            def iteration(it, f):
                for step in STEPS[f]:
                    kind = step[0]
                    g = INDEX[f].get(step)
                    if kind == "EXP":
                        n = step[1]
                        act.wait_ge(max_done.sem, max_done.value(it, n + 1))
                        fn(exp_bias[:, n % 4:n % 4 + 1], neg_max[:, n % 4:n % 4 + 1], ACT.Copy, scale=CH ** -0.5)\
                            .then_inc(bias_done.sem, 1)
                        act.wait_ge(bias_done.sem, bias_done.value(it, n + 1))
                        if n < 2 and f[2]:
                            for sent in out_sent[2 * n:2 * n + 2]:
                                act.wait_ge(sent.sem, sent.value(it, 2 * CB // RING))
                        if n >= 2:
                            act.wait_ge(pt_full.sem, pt_full.value(it, n - 1))
                        fn(probs[n % 2][:], scores[n % 2][:], ACT.Exp, bias=exp_bias[:, n % 4:n % 4 + 1],
                           scale=CH ** -0.5, accum_out=row_sum[:, n % 16:n % 16 + 1]).then_inc(exp_done.sem, 1)
                    elif kind == "T":
                        n = step[1]
                        act.wait_ge(pt_full.sem, pt_full.value(it, n + 1))
                        fn(pt[:, n % 2, :, n // 2 % 2 * P:(n // 2 % 2 + 1) * P], pt_ps[:], ACT.Copy)\
                            .then_inc(pt_copied.sem, 1)
                    elif kind == "WIDE":
                        c = step[1]
                        act.wait_ge(inv_done.sem, inv_done.value(it, c + 1))
                        fn(inv_wide[:], inv_sum[:, c % 2, :].unsqueeze(2).broadcast_to((P, 4, CH)), ACT.Copy)\
                            .then_inc(wide_done.sem, 1)
                    elif kind == "AV":
                        c = step[1]
                        act.wait_ge(product.sem, products(f, it, step))
                        fn(vy[:, c // 4, c % 4 * 2 * P:(c % 4 + 1) * 2 * P], bank[g % 2][:, 0:2 * P], ACT.Copy)\
                            .then_inc(emptied[g % 2].sem, 1)
                    elif kind == "SPREAD":
                        c = step[1]
                        act.wait_ge(product.sem, products(f, it, step))
                        if positive(norm_done.value(it, c)):
                            act.wait_ge(norm_done.sem, norm_done.value(it, c))
                        fn(inv_q[:], bank[g % 2][:, 0:2 * P], ACT.Copy).then_inc(emptied[g % 2].sem, 1)
                    elif kind == "VAR":
                        act.wait_ge(affine_done.sem, affine_done.value(it, 1))
                        for k in range(CB):
                            last = fn(u[:, k, :], u[:, k, :], ACT.Identity, scale=gn_a[:, k:k + 1],
                                      bias=gn_nb[:, k:k + 1])
                        last.then_inc(u_ready.sem, 1)
                    elif kind == "V":
                        act.wait_ge(product.sem, products(f, it, step))
                        tb = step[1]
                        fn(vy[:, 1:PAIRS + 1, tb * P:(tb + 1) * P],
                           bank[g % 2][:].rearrange("p (j c) -> p j c", j=PAIRS), ACT.Copy)\
                            .then_inc(emptied[g % 2].sem, 1)
                    elif kind == "QK":
                        _, j, t, h = step
                        act.wait_ge(product.sem, products(f, it, step))
                        fn(qk_raw[:, t, h * HALF:(h + 1) * HALF], bank[g % 2][:], ACT.Identity,
                           bias=qkb_sb[:, j, t:t + 1]).then_inc(emptied[g % 2].sem, 1)
                    elif kind == "SPLIT":
                        j = step[1]
                        if positive(scores_full.value(it, 2 * QB * j)):
                            act.wait_ge(scores_full.sem, scores_full.value(it, 2 * QB * j))
                        for which, count in copies(f, it, *[("QK", j, t, h) for t in range(2) for h in range(2)]):
                            act.wait_ge(emptied[which].sem, count)
                        for hd in range(2):
                            rows = slice(hd * CH, (hd + 1) * CH)
                            fn(k_st[0:CH, hd, 0, :], qk_raw[rows, 1, :], ACT.Copy)
                            fn(q_st[0:CH, hd, :], qk_raw[rows, 0, :], ACT.Copy).then_inc(high_done.sem, 1)
                            fn(k_st[CH:P, hd, 0, :], qk_raw[rows, 1, :], ACT.Copy)
                        for hd in range(2):
                            act.wait_ge(low_done.sem, low_done.value(it, 2 * j + hd + 1))
                            fn(k_st[CH:P, hd, 1, :], k_st[0:CH, hd, 1, :].bitcast(F32), ACT.Copy)\
                                .then_inc(twice_done.sem, 1)
                    elif kind == "P1":
                        _, m, h = step
                        t = m % 3
                        act.wait_ge(product.sem, products(f, it, step))
                        if m == BLOCKS - 1 and f[0]:
                            act.wait_ge(x1_sent.sem, x1_sent.value(it, 0))
                        if m >= 3:
                            act.wait_ge(conv_step.sem, conv_step.value(it, (m - 2) * CONV_STEPS))
                        rows = slice(PAD + h * H // 2, PAD + (h + 1) * H // 2)
                        src = bank[g % 2][:]
                        fn(pads[m % 3][:, rows, PAD:PAD + W], src.rearrange("p (a b) -> p a b", b=W), ACT.Copy)
                        dst = q_orig if t == 0 else kv_raw
                        fn(dst[:, h * HALF:(h + 1) * HALF], src, ACT.Copy if t == 2 else ACT.Relu)\
                            .then_inc(emptied[g % 2].sem, 1)
                    elif kind in ("PW", "TK", "TV", "TB"):
                        act.wait_ge(product.sem, products(f, it, step))
                        src = bank[g % 2][:]
                        h = step[-1]
                        cols = slice(h * HALF, (h + 1) * HALF)
                        src3 = src.rearrange("p (a b) -> p a b", b=P)
                        what = step[1] % 3 if kind == "PW" else {"TK": 1, "TV": 2, "TB": 3}[kind]
                        if what == 0:
                            last = fn(q_agg[:, cols], src, ACT.Relu)
                        elif what == 1:
                            last = fn(k_t[:, 4 * h:4 * h + 4, :], src3, ACT.Relu)
                        elif what == 2:
                            last = fn(v_t[:, 4 * h:4 * h + 4, 0:P], src3, ACT.Copy)
                        else:
                            last = fn(feat[:, SETS * step[1] + step[2], cols], src, ACT.Copy)
                        last.then_inc(emptied[g % 2].sem, 1)
                    elif step[0] == "COPY" and step[1][0] == "PROJ":
                        i = step[1][1]
                        ob, h = divmod(i, 2)
                        for which, count in copies(f, it, step[1]):
                            act.wait_ge(emptied[which].sem, count)
                        dst = out[bass.ds(it - 2, 1)] if not isinstance(it, int) else out[it - 2:it - 1]
                        dst = dst[:, ob * P:(ob + 1) * P, h * HALF:(h + 1) * HALF]
                        act.dma_start(dst.rearrange("a p t -> (a p) t"), part[i % RING])\
                            .then_inc(out_sent[i % RING].sem, 16)
                    elif step == ("COPY", ("OUT", 2 * CB - 1)):
                        for which, count in copies(f, it, ("OUT", 2 * CB - 2), ("OUT", 2 * CB - 1)):
                            act.wait_ge(emptied[which].sem, count)
                        dst = x1_dram[bass.ds(it, 1)] if not isinstance(it, int) else x1_dram[it:it + 1]
                        act.dma_start(dst.rearrange("a (k p) t -> p (a k) t", p=P), x1[:]).then_inc(x1_sent.sem, 16)
                if not f[0] and f[2]:
                    for sent in out_sent:
                        act.wait_ge(sent.sem, sent.value(it, 2 * CB // RING))

            iteration(0, BEGIN)
            iteration(1, SECOND)
            with act.Fori(2, NB) as it:
                iteration(it, STEADY)
            iteration(NB, DRAIN)
            iteration(NB + 1, END)

        @block.gpsimd
        def _(pool):
            pool.wait_ge(setup_dve, 1)
            with pool.Fori(0, NB) as it:
                pool.wait_ge(var_done.sem, it + 1)
                nc.gpsimd.tensor_tensor(gn[:, 3:4], gn[:, 4:5], gn[:, 5:6], ALU.pow).then_inc(std_done.sem, 1)

        @block.vector
        def _(dve):
            v = nc.vector
            for p in pads:
                v.memset(p[:], 0.0)
            v.memset(gn[:, 5:6], -0.5)
            v.memset(v_t[:, :, P:P + 1], 1.0).then_inc(setup_dve, 1)
            dve.wait_ge(const_in, 16 * 11)
            for m in range(BLOCKS):
                last = v.tensor_tensor(pw_bd[:, m, :].rearrange("p (h c) -> p h c", c=DIM),
                                       pw_dense[:, m, :].unsqueeze(1).broadcast_to((P, HEADS_SET, DIM)),
                                       bdmask[:].rearrange("p (h c) -> p h c", c=DIM), ALU.mult)
            last.then_inc(setup_dve, 1)
            dve.wait_ge(setup_pe, 1)
            v.tensor_tensor(outb2[:], scores[0][:, 0:CB], outb_sb[:], ALU.add).then_inc(setup_dve, 1)
            dve.wait_ge(setup_dve, 3)

            def iteration(it, f):
                links = [0]

                def link(ins):
                    links[0] += 1
                    ins.then_inc(link_done.sem, 1)
                    dve.wait_ge(link_done.sem, link_done.value(it, links[0]))

                for step in STEPS[f]:
                    if step[0] in BY_VECTOR:
                        continue
                    if step[0] == "COPY":
                        step = step[1]
                    kind = step[0]
                    g = INDEX[f].get(step)
                    if kind == "MAX":
                        n = step[1]
                        dve.wait_ge(scores_full.sem, scores_full.value(it, n + 1))
                        v.tensor_reduce(neg_max[:, n % 4:n % 4 + 1], scores[n % 2][:], AX_X, ALU.max, negate=True)\
                            .then_inc(max_done.sem, 1)
                    elif kind == "CONV":
                        _, m, i = step
                        if i == 0:
                            for which, count in copies(f, it, ("P1", m, 0), ("P1", m, 1)):
                                dve.wait_ge(emptied[which].sem, count)
                        full = acc[m % 2]
                        at = m * CONV_STEPS + i
                        if i == TAP_STEPS:
                            dve.wait_ge(conv_step.sem, conv_step.value(it, at))
                            v.tensor_tensor(full[:], full[:], side[:], ALU.add).then_inc(conv_step.sem, 1)
                            continue
                        dst = (full, side)[CHAIN[i]]
                        ty, tx = divmod(i, TAPS)
                        src = pads[m % 3][:, ty:ty + H, tx:tx + W]
                        wt = dw_sb[:, m, i:i + 1]
                        before = [k for k in range(i) if CHAIN[k] == CHAIN[i]]
                        if before:
                            dve.wait_ge(conv_step.sem, conv_step.value(it, m * CONV_STEPS + before[-1] + 1))
                            v.scalar_tensor_tensor(dst[:], src, wt, dst[:], ALU.mult, ALU.add)\
                                .then_inc(conv_step.sem, 1)
                        else:
                            if CHAIN[i] == 1:
                                if m > 0:
                                    dve.wait_ge(conv_step.sem, conv_step.value(it, m * CONV_STEPS))
                            elif m >= 2:
                                dve.wait_ge(product.sem, products(f, it, ("PW", m - 2, 1)))
                            v.tensor_scalar(dst[:], src, wt, None, ALU.mult).then_inc(conv_step.sem, 1)
                    elif kind == "STATS":
                        dve.wait_ge(x_in.sem, x_in.value(it, 1))
                        for i in range(2 * CB):
                            last = v.bn_stats(bn6[:, i, :], u[:, i // 2, i % 2 * HALF:(i % 2 + 1) * HALF])
                        link(last)
                        v.tensor_copy(gn[:, 6:7], gn[:, 5:6])
                        v.bn_aggr(mv[:], bn6[:].rearrange("p a b -> p (a b)")).then_inc(stats_done.sem, 1)
                    elif kind == "MEAN":
                        dve.wait_ge(product.sem, products(f, it, step))
                        ps = bank[g % 2][:, 0:1]
                        link(v.tensor_tensor(gn[:, 0:1], mv[:, 0:1], ps, ALU.subtract))
                        v.tensor_copy(gn[:, 2:3], ps).then_inc(emptied[g % 2].sem, 1)
                        v.tensor_scalar(gn[:, 1:2], gn[:, 0:1], gn[:, 0:1], mv[:, 1:2], ALU.mult, ALU.add)\
                            .then_inc(stats_done.sem, 1)
                    elif kind == "VAR":
                        dve.wait_ge(product.sem, products(f, it, step))
                        for which, count in copies(f, it, ("MEAN",)):
                            dve.wait_ge(emptied[which].sem, count)
                        v.tensor_scalar(gn[:, 4:5], bank[g % 2][:, 0:1], GN_EPS, None, ALU.add)\
                            .then_inc(var_done.sem, 1)
                        dve.wait_ge(std_done.sem, std_done.value(it, 1))
                        link(v.tensor_scalar(gn_a[:], gnw_sb[:], gn[:, 3:4], None, ALU.mult))
                        v.tensor_copy(gn[:, 0:1], bank[g % 2][:, 0:1]).then_inc(emptied[g % 2].sem, 1)
                        link(v.tensor_scalar(gn_nb[:], gn_a[:], gn[:, 2:3], None, ALU.mult))
                        v.tensor_tensor(gn_nb[:], gnb_sb[:], gn_nb[:], ALU.subtract).then_inc(affine_done.sem, 1)
                    elif kind == "SPLIT":
                        j = step[1]
                        for hd in range(2):
                            dve.wait_ge(high_done.sem, high_done.value(it, 2 * j + hd + 1))
                            rows = slice(hd * CH, (hd + 1) * CH)
                            v.tensor_tensor(k_st[0:CH, hd, 1, :], qk_raw[rows, 1, :],
                                            k_st[0:CH, hd, 0, :].bitcast(F32), ALU.subtract)
                            v.tensor_tensor(q_st[CH:P, hd, :], qk_raw[rows, 0, :],
                                            q_st[0:CH, hd, :].bitcast(F32), ALU.subtract).then_inc(low_done.sem, 1)
                    elif kind == "RECIP":
                        c = step[1]
                        dve.wait_ge(exp_done.sem, exp_done.value(it, 4 * c + 4))
                        v.reciprocal(inv_sum[:, c % 2, :], row_sum[:, 4 * c % 16:4 * c % 16 + 4])\
                            .then_inc(inv_done.sem, 1)
                    elif kind == "NORM":
                        c = step[1]
                        for which, count in copies(f, it, ("AV", c), ("SPREAD", c)):
                            dve.wait_ge(emptied[which].sem, count)
                        y = vy[:, c // 4, c % 4 * 2 * P:(c % 4 + 1) * 2 * P]
                        v.tensor_tensor(y, y, inv_q[:], ALU.mult).then_inc(norm_done.sem, 1)
                    elif kind == "VK":
                        dve.wait_ge(product.sem, products(f, it, step))
                        ps = bank[g % 2]
                        v.tensor_tensor(vk[:, 0:P], ps[:, 0:P], bdmask[:], ALU.mult)
                        v.tensor_scalar(vk[:, P:NW], hmask[:], ps[:, P:P + 1], None, ALU.mult)\
                            .then_inc(emptied[g % 2].sem, 1)
                    elif kind == "NUM":
                        _, s, j, g3 = step
                        dve.wait_ge(product.sem, products(f, it, step))
                        nb = min(QB, 3 * g3 + 3) - 3 * g3
                        ps = bank[g % 2][:, 0:nb * NW].rearrange("p (a b) -> p a b", b=NW)
                        d = [den[:, g % 2, i, 0:nb * HEADS_SET].rearrange("p (a b) -> p a b", b=HEADS_SET)
                             for i in range(2)]
                        link(v.tensor_scalar(d[0], ps[:, :, P:NW], ATT_EPS, None, ALU.add))
                        link(v.reciprocal(d[1], d[0]))
                        v.tensor_tensor(num_t[:, 3 * g3:3 * g3 + nb, :].rearrange("p a (h c) -> p a h c", c=DIM),
                                        ps[:, :, 0:P].rearrange("p a (h c) -> p a h c", c=DIM),
                                        d[1].unsqueeze(3).broadcast_to((P, nb, HEADS_SET, DIM)), ALU.mult)\
                            .then_inc(emptied[g % 2].sem, 1)
                    elif kind == "PROJ":
                        i = step[1]
                        ob, h = divmod(i, 2)
                        dve.wait_ge(product.sem, products(f, it, step))
                        dve.wait_ge(res_in[i % RING].sem, res_in[i % RING].value(it, i // RING + 1))
                        v.tensor_tensor(part[i % RING], bank[g % 2][:], part[i % RING], ALU.add)\
                            .then_inc(emptied[g % 2].sem, 1)
                    elif kind == "OUT":
                        h, ob = divmod(step[1], CB)
                        dve.wait_ge(product.sem, products(f, it, step))
                        if step[1] == 0:
                            dve.wait_ge(x_again_in.sem, x_again_in.value(it, 1))
                        cols = slice(h * HALF, (h + 1) * HALF)
                        v.scalar_tensor_tensor(x1[:, ob, cols], bank[g % 2][:], outb2[:, ob:ob + 1],
                                               x1[:, ob, cols], ALU.add, ALU.add).then_inc(emptied[g % 2].sem, 1)
                assert links[0] == (LINKS0 if f[0] else 0) + (LINKS1 if f[1] else 0), links

            iteration(0, BEGIN)
            iteration(1, SECOND)
            with dve.Fori(2, NB) as it:
                iteration(it, STEADY)
            iteration(NB, DRAIN)
            iteration(NB + 1, END)


def kernel(x, L0_conv_gn_weight, L0_conv_gn_bias, L0_conv_qkv_w, L0_conv_qkv_b, L0_conv_out_w, L0_conv_out_b,
           L1_conv_w_qkv, L1_conv_w_dw, L1_conv_w_pw, L1_conv_w_proj):
    import concourse.bacc as bacc
    from concourse.bass_utils import run_bass_kernel_spmd

    def lay(a):
        return np.ascontiguousarray(a)

    def per_block(a):
        return lay(np.asarray(a).reshape(-1, P).T)

    x, qkv_w, qkv_b = np.asarray(x), np.asarray(L0_conv_qkv_w), np.asarray(L0_conv_qkv_b)
    w_t = qkv_w.T.reshape(CB, P, 3, PAIRS, P)
    order = np.arange(3 * C).reshape(SETS, HEADS_SET, 3, DIM).transpose(0, 2, 1, 3).reshape(-1)
    w1 = np.asarray(L1_conv_w_qkv).reshape(3 * C, C)[order].reshape(SETS, 3, P, CB, P)
    arrays = {
        "x": lay(x.reshape(NB, C, L)),
        "w0qk": lay(w_t[:, :, 0:2].transpose(3, 1, 0, 2, 4)),
        "w0v": lay(w_t[:, :, 2].reshape(CB, P, C).transpose(1, 0, 2)),
        "w0out": lay(np.asarray(L0_conv_out_w).T.reshape(CB, P, C).transpose(1, 0, 2)),
        "w1": lay(w1.transpose(0, 4, 3, 1, 2)),
        "wproj": lay(np.asarray(L1_conv_w_proj).reshape(C, 2 * C).T.reshape(2 * SETS, P, C).transpose(1, 0, 2)),
        "pw": lay(np.asarray(L1_conv_w_pw).reshape(3 * C, DIM)[order].reshape(BLOCKS, HEADS_SET, DIM, DIM)
                  .transpose(1, 3, 0, 2).reshape(P, BLOCKS, DIM)),
        "dw": lay(np.asarray(L1_conv_w_dw).reshape(3 * C, TAPS * TAPS)[order].reshape(BLOCKS, P, -1)
                  .transpose(1, 0, 2)),
        "gnw": per_block(L0_conv_gn_weight),
        "gnb": per_block(L0_conv_gn_bias),
        "qk_bias": lay(qkv_b[:2 * C].reshape(2, PAIRS, P).transpose(2, 1, 0)),
        "v_bias": per_block(qkv_b[2 * C:]),
        "out_bias": per_block(L0_conv_out_b),
        "identity": np.eye(P, dtype=np.float32),
        "block_mask": np.kron(np.eye(HEADS_SET), np.ones((DIM, DIM))).astype(np.float32),
        "head_mask": np.kron(np.eye(HEADS_SET), np.ones((DIM, 1))).astype(np.float32),
        "ones": np.full((P, P), 1.0 / P, np.float32),
    }
    nc = bacc.Bacc("TRN2", target_bir_lowering=False, num_devices=1, dynamic_dma_scratch_size=1024)
    args = {n: nc.dram_tensor(f"in_{n}", a.shape, F32, kind="ExternalInput").ap() for n, a in arrays.items()}
    out = nc.dram_tensor("out_0", (NB, C, L), F32, kind="ExternalOutput").ap()
    build(nc, out=out, **args)
    r = run_bass_kernel_spmd(nc, [{f"in_{n}": a for n, a in arrays.items()}], core_ids=[0])
    return r.results[0]["out_0"].reshape(NB, C, H, W)
```

```python
from contextlib import ExitStack

import numpy as np
import concourse.bass as bass
from concourse import mybir

P = 128
F32 = mybir.dt.float32
F32R = mybir.dt.float32r
ALU = mybir.AluOpType
ACT = mybir.ActivationFunctionType
AX_X = mybir.AxisListType.X

NB, C, H, W = 8, 512, 32, 32
L = H * W
CB = C // P
NHEAD, CH = 8, 64
PAIRS = NHEAD // 2
QB = L // P
GN_EPS = 1e-5
TAPS = 5
PAD = TAPS // 2
HP = H + 2 * PAD
DIM = 8
HEADS_SET = P // DIM
SETS = C // P
BLOCKS = 3 * SETS
ATT_EPS = 1e-15
HALF = 512
UNITS = NHEAD * QB
NW = P + HEADS_SET

QK_AT = (6, 8, 10, 12)
FILL_FIRST, FILL_LAST = 17, 7
RING = 4

TAP_STEPS = TAPS * TAPS
CONV_STEPS = TAP_STEPS + 1
CHAIN = [1 if i < 3 else (0 if i % 2 else 1) for i in range(TAP_STEPS)]
BY_SCALAR = CHAIN.index(0)
BY_TENSOR = (6, 8, 10, 14, 16, 18, 22)
CHUNK = [6, 5, 5, 5, 5]


def vector_taps(alone):
    return [i for i in range(TAP_STEPS) if i != BY_SCALAR and not (alone and i in BY_TENSOR)]


def vector_steps(alone):
    return len(vector_taps(alone)) + (2 if alone else 1)


def layer1_chunks():
    chunks = []
    for m in range(BLOCKS + 1):
        j, t = divmod(m, 3)
        window = [[] for _ in CHUNK]
        if t != 2 and m < BLOCKS:
            window[1].append(("P1", m + 1, 0))
            window[3].append(("P1", m + 1, 1))
        if t == 1:
            window[0] += [("PW", m - 1, 0), ("PW", m - 1, 1), ("TK", j, 0)]
            window[1] += [("TK", j, 1)]
            if m > 1:
                window[2] += [("TB", 1, j - 1, h) for h in range(2)]
            window[4] += [("TV", j, 0), ("TV", j, 1)]
        if t == 2:
            window[0] += [("VK", 0, j)]
            window[1] += [("NUM", 0, j, 0), ("NUM", 0, j, 1)]
            window[2] += [("NUM", 0, j, 2), ("PW", m - 1, 0)]
            window[3] += [("PW", m - 1, 1)]
            if m + 1 < BLOCKS:
                window[2].insert(1, ("P1", m + 1, 0))
                window[3].append(("P1", m + 1, 1))
            window[4] += [("TB", 0, j, h) for h in range(2)]
        if t == 0 and m > 0:
            last = m == BLOCKS
            window[0] += [("PW", m - 1, 0), ("PW", m - 1, 1)]
            window[2] += [("VK", 1, j - 1)]
            window[3] += [("NUM", 1, j - 1, 0)]
            window[4] += [("NUM", 1, j - 1, 1), ("NUM", 1, j - 1, 2)]
            if last:
                window[4] += [("TB", 1, j - 1, h) for h in range(2)]
        for r, groups in enumerate(window):
            lo = sum(CHUNK[:r])
            steps = [("CONV", m, i) for i in range(lo, lo + CHUNK[r])] if m < BLOCKS else []
            if groups or steps:
                chunks.append((groups, steps))
    return chunks


BANKS = 4
GROUPS = ("P1", "T", "V", "QK", "PW", "TK", "TV", "VK", "NUM", "TB", "AV", "SPREAD", "PROJ", "OUT")
BY_VECTOR = ("VK", "NUM", "PROJ", "OUT")


def timeline(l0, l1, l2):
    chunks = layer1_chunks() if l1 else []
    if l1 and not l0:
        for m in range(BLOCKS):
            chunks[m * len(CHUNK)][1].insert(0, ("TAPS", m, 0))
            chunks[m * len(CHUNK) + 3][1].insert(4, ("TAPS", m, 1))
    done, out = [0], []

    def add(groups, steps):
        steps, late, lag = list(steps), [], 1
        per = -(-len(steps) // max(1, len(groups)))
        for g in groups:
            out.append(g)
            part, steps = steps[:per], steps[per:]
            out.extend(part[:lag] + late + part[lag:])
            late = [("COPY", g)] if g[0] in BY_VECTOR else []
            lag = 1 if l0 else 4
        out.extend(steps[:lag] + late + steps[lag:])

    def take(upto):
        groups, steps = [], []
        while done[0] < min(upto, len(chunks)):
            groups += chunks[done[0]][0]
            steps += chunks[done[0]][1]
            done[0] += 1
        return groups, steps

    if l1:
        out += [("P1", 0, 0), ("P1", 0, 1)]
    if l0:
        out.append(("STATS",))
    first = [("PROJ", i) for i in range(2 * CB)] if l2 else []
    if l0:
        first.insert(min(1, len(first)), ("MEAN",))
        first.insert(min(3, len(first)), ("VAR",))
        first += [("V", i) for i in range(QB)] + [("QK", 0, t, h) for t in (1, 0) for h in range(2)]
    fill = FILL_FIRST if l0 else 13
    for i, step in enumerate(first):
        g, s = take((i + 1) * fill // len(first))
        add([step] + g, s)
    if l0:
        out += [("HIGH", 0, 0), ("LOW", 0, 0), ("TWICE", 0, 0), ("HIGH", 0, 1), ("S", 0), ("LOW", 0, 1), ("TWICE", 0, 1),
                ("MAX", 0), ("EXP", 0)]
        rest = len(chunks) - done[0] - FILL_LAST
        begun = done[0]
        span = 2 * QB
        for n in range(UNITS):
            g, s = take(begun + (n + 1) * rest // UNITS if l1 else 0)
            nxt = n + 1 < UNITS
            j, at = divmod(n, span)
            if j + 1 < PAIRS and at in QK_AT:
                r = QK_AT.index(at)
                g = [("QK", j + 1, 1 - r // 2, r % 2)] + g
            c = n // 4
            scaling = [[("RECIP", c - 1)], [("WIDE", c - 1)], [("SPREAD", c - 1)], [("NORM", c - 1)]][n % 4] if c else []
            k = len(s) // 2
            if nxt and at == span - 1:
                out += [("HIGH", j + 1, 0), ("T", n, 0), ("T", n, 1)]
                add(g[:1], s[:1])
                out += [("LOW", j + 1, 0), ("TWICE", j + 1, 0), ("AV", c), ("HIGH", j + 1, 1), ("COPY", ("AV", c))]
                add(g[1:], s[1:k])
                out += [("S", n + 1), ("LOW", j + 1, 1), ("TWICE", j + 1, 1), ("MAX", n + 1)] + scaling
                out += [("EXP", n + 1)] + s[max(k, 1):]
                continue
            if nxt:
                out.append(("S", n + 1))
            add(g[:len(g) // 2], s[:k])
            if nxt:
                out.append(("MAX", n + 1))
            add(g[len(g) // 2:], s[k:-1])
            out += scaling
            if n % 4 == 0 and at > 0:
                out.append(("AV", c - 1))
            if nxt:
                out.append(("EXP", n + 1))
            out += s[-1:]
            if n % 4 == 0 and at > 0:
                out.append(("COPY", ("AV", c - 1)))
            out += [("T", n, 0), ("T", n, 1)]
        c = UNITS // 4 - 1
        out += [("AV", c), ("COPY", ("AV", c)), ("RECIP", c), ("WIDE", c)]
        for i in range(2 * CB):
            if i == CB - 2:
                out += [("SPREAD", c), ("NORM", c)]
            g, s = take(done[0] + 1 if i % 2 else 0)
            add([("OUT", i)] + g, s)
    while done[0] < len(chunks):
        g, s = take(done[0] + 1)
        add(g, s)
    return out


def build(nc, x, w0qk, w0v, w0out, w1, wproj, pw, dw, gnw, gnb, qk_bias, v_bias, out_bias,
          identity, block_mask, head_mask, ones, out):
    FLAGS = [(True, False, False), (True, True, False), (True, True, True), (False, True, True), (False, False, True)]
    BEGIN, SECOND, STEADY, DRAIN, END = FLAGS
    STEPS = {f: timeline(*f) for f in FLAGS}
    INDEX = {}
    for f, steps in STEPS.items():
        INDEX[f] = {s: i for i, s in enumerate([s for s in steps if s[0] in GROUPS])}
    G0, G2 = len(INDEX[BEGIN]), len(INDEX[END])
    G1 = len(INDEX[SECOND]) - G0
    assert len(INDEX[STEADY]) == G0 + G1 + G2 and G0 % BANKS == 0 and G1 % BANKS == 0 and G2 % BANKS == 0

    x1_dram = nc.dram_tensor("x1_dram", (NB, C, L), F32, kind="Internal").ap()
    ctx = ExitStack()
    with ctx:
        def sb(name, shape, dt=F32):
            return ctx.enter_context(nc.sbuf_tensor(name, shape, dt))

        def psum(name, shape):
            return ctx.enter_context(nc.psum_tensor(name, shape, F32))

        def sem(name):
            return ctx.enter_context(nc.semaphore(name))

        class Signal:

            def __init__(self, name, l0, l1, l2=0, by=1):
                self.sem, self.l0, self.l1, self.l2, self.by = sem(name), l0, l1, l2, by

            def value(self, it, n):
                if isinstance(it, int):
                    k = self.l0 * min(it, NB) + self.l1 * min(max(it - 1, 0), NB) + self.l2 * max(it - 2, 0)
                    return (k + n) * self.by
                return it * ((self.l0 + self.l1 + self.l2) * self.by) + (n - self.l1 - 2 * self.l2) * self.by

        def positive(v):
            return not (isinstance(v, int) and v <= 0)

        w_small = sb("w_small", [P, CB, C])
        w0qk_sb = sb("w0qk_sb", [P, CB, 2, P])
        w1_sb = sb("w1_sb", [P, CB, 3, P])
        pw_dense = sb("pw_dense", [P, BLOCKS, DIM])
        pw_bd = sb("pw_bd", [P, BLOCKS, P])
        dw_sb = sb("dw_sb", [P, BLOCKS, TAPS * TAPS])
        gnw_sb = sb("gnw_sb", [P, CB])
        gnb_sb = sb("gnb_sb", [P, CB])
        qkb_sb = sb("qkb_sb", [P, PAIRS, 2])
        vb_sb = sb("vb_sb", [P, PAIRS])
        outb_sb = sb("outb_sb", [P, CB])
        outb2 = sb("outb2", [P, CB])
        ident = sb("ident", [P, P])
        bdmask = sb("bdmask", [P, P])
        hmask = sb("hmask", [P, HEADS_SET])
        mean_w = sb("mean_w", [P, P])
        u = sb("u", [P, CB, L])
        qk_raw = sb("qk_raw", [P, 2, L])
        q_st = sb("q_st", [P, 2, L], F32R)
        k_st = sb("k_st", [P, 2, 2, L], F32R)
        vy = sb("vy", [P, PAIRS + 1, L])
        probs = [sb(f"probs{i}", [P, L]) for i in range(2)]
        pt = sb("pt", [P, 2, QB, 2 * P])
        x1 = sb("x1", [P, CB, L])
        pads = [sb(f"pad{i}", [P, HP, HP]) for i in range(3)]
        acc = [sb(f"acc{i}", [P, H, W]) for i in range(2)]
        side = sb("side", [P, H, W])
        q_orig = sb("q_orig", [P, L])
        q_agg = sb("q_agg", [P, L])
        kv_raw = sb("kv_raw", [P, L])
        k_t = sb("k_t", [P, QB, P])
        v_t = sb("v_t", [P, QB, P + 1])
        vk = sb("vk", [P, NW])
        den = sb("den", [P, 2, 2, 3 * HEADS_SET])
        num_t = sb("num_t", [P, QB, P])
        feat = sb("feat", [P, 2 * SETS, L])
        row_sum = sb("row_sum", [P, 16])
        inv_sum = sb("inv_sum", [P, 2, 4])
        inv_wide = sb("inv_wide", [P, 4, CH])
        inv_q = sb("inv_q", [P, 2 * P])
        neg_max = sb("neg_max", [P, 4])
        exp_bias = sb("exp_bias", [P, 4])
        bn6 = sb("bn6", [P, 2 * CB, 6])
        mv = sb("mv", [P, 2])
        gn = sb("gn", [P, 7])
        gn_a = sb("gn_a", [P, CB])
        gn_nb = sb("gn_nb", [P, CB])
        wproj_sb = pt[:, :, :, :].rearrange("p a b c -> p (a b c)").rearrange("p (b n) -> p b n", b=2 * SETS)
        diagonal = u[:].rearrange("p k t -> p (k t)").rearrange("p (a i c) -> p a i c", a=2, c=P)
        part = [probs[i // 2][:, i % 2 * HALF:(i % 2 + 1) * HALF] for i in range(RING)]

        scores = [psum(f"scores{i}", [P, L]) for i in range(2)]
        bank = [psum(f"bank{i}", [P, HALF]) for i in range(BANKS)]

        const_in = sem("const_in")
        w0out_pre = sem("w0out_pre")
        setup_dve = sem("setup_dve")
        setup_pe = sem("setup_pe")
        x_in = Signal("x_in", 1, 0, 0, 16)
        w0v_in = Signal("w0v_in", 1, 0, 0, 16)
        w0qk_in = Signal("w0qk_in", PAIRS, 0, 0, 16)
        w0out_in = Signal("w0out_in", 1, 0, 0, 16)
        w1_in = Signal("w1_in", 0, SETS, 0, 16)
        wproj_in = Signal("wproj_in", 0, 1, 0, 16)
        res_in = [Signal(f"res_in{i}", 0, 0, 2 * CB // RING, 16) for i in range(RING)]
        x_again_in = Signal("x_again_in", 1, 0, 0, 16)
        x1_sent = Signal("x1_sent", 1, 0, 0, 16)
        out_sent = [Signal(f"out_sent{i}", 0, 0, 2 * CB // RING, 16) for i in range(RING)]
        product = Signal("product", G0, G1, G2)
        emptied = [Signal(f"emptied{i}", G0 // BANKS, G1 // BANKS, G2 // BANKS) for i in range(BANKS)]
        scores_full = Signal("scores_full", UNITS, 0)
        max_done = Signal("max_done", UNITS, 0)
        bias_done = Signal("bias_done", UNITS, 0)
        exp_done = Signal("exp_done", UNITS, 0)
        sums_full = Signal("sums_full", 2, 0)
        inv_done = Signal("inv_done", UNITS // 4, 0)
        wide_done = Signal("wide_done", UNITS // 4, 0)
        norm_done = Signal("norm_done", UNITS // 4, 0)
        high_done = Signal("high_done", 4 * PAIRS, 0)
        low_done = Signal("low_done", 4 * PAIRS, 0)
        twice_done = Signal("twice_done", 2 * PAIRS, 0)
        affine_done = Signal("affine_done", 1, 0)
        stats_done = Signal("stats_done", 2, 0)
        var_done = Signal("var_done", 1, 0)
        std_done = Signal("std_done", 1, 0)
        u_ready = Signal("u_ready", 1, 0)
        conv_step = Signal("conv_step", 0, BLOCKS * vector_steps(False))
        tap_done = Signal("tap_done", 0, BLOCKS)
        diagonals_done = sem("diagonals_done")
        taps_full = sem("taps_full")
        LINKS0, LINKS1 = 4, 2 * SETS * 3 * 2
        link_done = Signal("link_done", LINKS0, LINKS1)

        def products(f, it, step):
            return product.value(it, INDEX[f][step] + 1)

        def copies(f, it, *steps):
            last = {}
            for g in sorted(INDEX[f][s] for s in steps):
                last[g % BANKS] = g
            return [(b, emptied[b].value(it, g // BANKS + 1)) for b, g in last.items()]

        block = ctx.enter_context(nc.Block())

        @block.sync
        def _(sp):
            def load_x(it):
                src = x[bass.ds(it, 1)] if not isinstance(it, int) else x[it:it + 1]
                sp.dma_start(u[:], src.rearrange("a (k p) t -> p (a k) t", p=P)).then_inc(x_in.sem, 16)

            load_x(0)
            for dst, src in ((pw_dense, pw), (dw_sb, dw), (gnw_sb, gnw), (gnb_sb, gnb), (qkb_sb, qk_bias),
                             (vb_sb, v_bias), (outb_sb, out_bias), (ident, identity), (bdmask, block_mask),
                             (hmask, head_mask), (mean_w, ones)):
                sp.dma_start(dst[:], src).then_inc(const_in, 16)

            def load_x_again(it):
                src = x[bass.ds(it, 1)] if not isinstance(it, int) else x[it:it + 1]
                sp.dma_start(x1[:], src.rearrange("a (k p) t -> p (a k) t", p=P)).then_inc(x_again_in.sem, 16)

            def load_w0v(it):
                sp.wait_ge(product.sem, product.value(it, 0))
                sp.dma_start(w_small[:], w0v).then_inc(w0v_in.sem, 16)

            def load_w0qk(j):
                sp.dma_start(w0qk_sb[:], w0qk[j]).then_inc(w0qk_in.sem, 16)

            def load_w1(j):
                sp.dma_start(w1_sb[:], w1[j]).then_inc(w1_in.sem, 16)

            sp.dma_start(w_small[:], w0v).then_inc(w0v_in.sem, 16)
            load_w0qk(0)
            load_w1(0)
            sp.dma_start(wproj_sb[:, 0:CB, :], w0out).then_inc(w0out_pre, 16)

            def image(t, i):
                return t[i:i + 1] if isinstance(i, int) else t[bass.ds(i, 1)]

            def iteration(it, f, more, before=None):
                l0, l1, l2 = f
                last_image = it - 2 if isinstance(it, int) else sp.snap(it - 2)
                if l2:
                    if f == END:
                        sp.wait_ge(x1_sent.sem, x1_sent.value(it - 1, 0))
                    else:
                        after = G0 + G1 + (G2 if before[2] else 0) - INDEX[before][("T", UNITS - 1, 1)] - 1
                        sp.wait_ge(product.sem, product.value(it, -after))
                    for i in range(2 * CB):
                        if i == RING and l0:
                            load_w0v(it)
                        if i >= RING or f == END:
                            sp.wait_ge(out_sent[i % RING].sem, out_sent[i % RING].value(it, i // RING))
                        ob, h = divmod(i, 2)
                        src = image(x1_dram, last_image)[:, ob * P:(ob + 1) * P, h * HALF:(h + 1) * HALF]
                        sp.dma_start(part[i % RING], src.rearrange("a p t -> (a p) t")).then_inc(res_in[i % RING].sem, 16)
                elif l0 and l1:
                    load_w0v(it)
                loads = []
                if l0:
                    loads.append((("V", QB - 1), "w0out", 0))
                    loads += [(("QK", j, 0, 1), "w0qk", j + 1) for j in range(PAIRS) if j + 1 < PAIRS or more]
                    if l1:
                        loads.append((("P1", BLOCKS - 1, 1), "x", 0))
                    else:
                        load_x_again(it)
                if l1:
                    loads += [(("P1", 3 * j + 2, 1), "w1", j + 1) for j in range(SETS) if j + 1 < SETS or l0]
                for user, what, j in sorted(loads, key=lambda load: INDEX[f][load[0]]):
                    if what == "x":
                        for which, count in copies(f, it, user):
                            sp.wait_ge(emptied[which].sem, count)
                        load_x_again(it)
                        continue
                    sp.wait_ge(product.sem, products(f, it, user))
                    if what == "w0out":
                        sp.dma_start(w_small[:], w0out).then_inc(w0out_in.sem, 16)
                    elif what == "w1":
                        load_w1(j % SETS)
                    else:
                        load_w0qk(j % PAIRS)
                        if j == PAIRS:
                            load_x(it + 1)
                if l1:
                    if l0:
                        sp.wait_ge(product.sem, products(f, it, ("AV", UNITS // 4 - 1)))
                    elif l2:
                        sp.wait_ge(product.sem, products(f, it, ("PROJ", 2 * CB - 1)))
                    sp.dma_start(wproj_sb[:], wproj).then_inc(wproj_in.sem, 16)

            iteration(0, BEGIN, True)
            iteration(1, SECOND, True)
            with sp.Fori(2, NB - 1) as it:
                iteration(it, STEADY, True, STEADY)
            iteration(NB - 1, STEADY, False, STEADY)
            iteration(NB, DRAIN, False, STEADY)
            iteration(NB + 1, END, False)

        @block.tensor
        def _(pe):
            mm = nc.tensor.matmul
            pe.wait_ge(const_in, 16 * 11)
            pe.wait_ge(w0out_pre, 16)
            for ob in range(CB):
                for j in range(PAIRS):
                    last = mm(scores[0][:, ob:ob + 1], wproj_sb[:, j, ob * P:(ob + 1) * P], vb_sb[:, j:j + 1],
                              start=(j == 0), stop=(j == PAIRS - 1))
            last.then_inc(setup_pe, 1)
            pe.wait_ge(setup_dve, 3)

            def group(it, f, step):
                g = INDEX[f][step]
                b = bank[g % BANKS]
                if positive(emptied[g % BANKS].value(it, g // BANKS)):
                    pe.wait_ge(emptied[g % BANKS].sem, emptied[g % BANKS].value(it, g // BANKS))
                kind = step[0]
                if kind == "T":
                    _, n, h = step
                    if h == 0:
                        pe.wait_ge(exp_done.sem, exp_done.value(it, n + 1))
                    for i in range(4):
                        kb = 4 * h + i
                        last = nc.tensor.transpose(b[:, i * P:(i + 1) * P], probs[n % 2][:, kb * P:(kb + 1) * P], ident[:])
                elif kind == "V":
                    tb = step[1]
                    if tb == 0:
                        pe.wait_ge(u_ready.sem, u_ready.value(it, 1))
                        pe.wait_ge(w0v_in.sem, w0v_in.value(it, 1))
                    for k in range(CB):
                        last = mm(b[:], u[:, k, tb * P:(tb + 1) * P], w_small[:, k, :],
                                  start=(k == 0), stop=(k == CB - 1))
                elif kind == "QK":
                    _, j, t, h = step
                    if t == 1 and h == 0:
                        pe.wait_ge(w0qk_in.sem, w0qk_in.value(it, j + 1))
                    for k in range(CB):
                        last = mm(b[:], w0qk_sb[:, k, t, :], u[:, k, h * HALF:(h + 1) * HALF],
                                  start=(k == 0), stop=(k == CB - 1))
                elif kind == "AV":
                    c = step[1]
                    j = c // 4
                    for which, count in copies(f, it, ("T", 4 * c + 3, 0), ("T", 4 * c + 3, 1)):
                        pe.wait_ge(emptied[which].sem, count)
                    if c == 0:
                        for which, count in copies(f, it, ("V", QB - 2), ("V", QB - 1)):
                            pe.wait_ge(emptied[which].sem, count)
                    for kb in range(QB):
                        for hd in range(2):
                            last = mm(b[hd * CH:(hd + 1) * CH, 0:2 * P],
                                      vy[:, j + 1, kb * P + hd * CH:kb * P + (hd + 1) * CH],
                                      pt[:, hd, kb, :], start=(kb == 0), stop=(kb == QB - 1))
                elif kind == "SPREAD":
                    c = step[1]
                    pe.wait_ge(wide_done.sem, wide_done.value(it, c + 1))
                    for q in range(2):
                        last = nc.tensor.transpose(b[:, q * P:(q + 1) * P],
                                                   inv_wide[:, 2 * q:2 * q + 2, :].rearrange("p a c -> p (a c)"),
                                                   ident[:])
                elif kind == "OUT":
                    h, ob = divmod(step[1], CB)
                    if step[1] == 0:
                        pe.wait_ge(w0out_in.sem, w0out_in.value(it, 1))
                    if ob == 0:
                        pe.wait_ge(norm_done.sem, norm_done.value(it, UNITS // 4 - 2 * (1 - h)))
                    for j in range(PAIRS):
                        last = mm(b[:], w_small[:, j, ob * P:(ob + 1) * P], vy[:, j, h * HALF:(h + 1) * HALF],
                                  start=(j == 0), stop=(j == PAIRS - 1))
                elif kind == "P1":
                    _, m, h = step
                    j, t = divmod(m, 3)
                    if h == 0 and t == 0:
                        pe.wait_ge(w1_in.sem, w1_in.value(it, j + 1))
                    if h == 0 and m == 0:
                        for i in range(BANKS):
                            pe.wait_ge(emptied[i].sem, emptied[i].value(it, 0))
                    for k in range(CB):
                        last = mm(b[:], w1_sb[:, k, t, :], x1[:, k, h * HALF:(h + 1) * HALF],
                                  start=(k == 0), stop=(k == CB - 1))
                elif kind == "PW":
                    _, m, h = step
                    if h == 0:
                        pe.wait_ge(conv_step.sem, conv_step.value(it, (m + 1) * vector_steps(f == DRAIN)))
                    a = acc[m % 2][:].rearrange("p a b -> p (a b)")
                    if m % 3 == 0:
                        last = mm(b[:], pw_bd[:, m, :], a[:, h * HALF:(h + 1) * HALF], start=True, stop=True)
                    else:
                        for i in range(4):
                            tb = 4 * h + i
                            last = mm(b[:, i * P:(i + 1) * P], a[:, tb * P:(tb + 1) * P], pw_bd[:, m, :],
                                      start=True, stop=True)
                elif kind in ("TK", "TV"):
                    _, j, h = step
                    for which, count in copies(f, it, ("P1", 3 * j + (1 if kind == "TK" else 2), h)):
                        pe.wait_ge(emptied[which].sem, count)
                    for i in range(4):
                        tb = 4 * h + i
                        last = nc.tensor.transpose(b[:, i * P:(i + 1) * P], kv_raw[:, tb * P:(tb + 1) * P], ident[:])
                elif kind == "VK":
                    _, s, j = step
                    if s == 0:
                        for which, count in copies(f, it, *[(kind, j, h) for kind in ("TK", "TV") for h in range(2)]):
                            pe.wait_ge(emptied[which].sem, count)
                    else:
                        for which, count in copies(f, it, *[("PW", 3 * j + t, h) for t in (1, 2) for h in range(2)]):
                            pe.wait_ge(emptied[which].sem, count)
                    for tb in range(QB):
                        last = mm(b[:, 0:P + 1], k_t[:, tb, :], v_t[:, tb, :], start=(tb == 0), stop=(tb == QB - 1))
                elif kind == "NUM":
                    _, s, j, g3 = step
                    if g3 == 0:
                        queries = "P1" if s == 0 else "PW"
                        for which, count in copies(f, it, ("VK", s, j), (queries, 3 * j, 0), (queries, 3 * j, 1)):
                            pe.wait_ge(emptied[which].sem, count)
                    q = q_orig if s == 0 else q_agg
                    for i, tb in enumerate(range(3 * g3, min(QB, 3 * g3 + 3))):
                        last = mm(b[:, i * NW:(i + 1) * NW], q[:, tb * P:(tb + 1) * P], vk[:], start=True, stop=True)
                elif kind == "TB":
                    _, s, j, h = step
                    for which, count in copies(f, it, *[("NUM", s, j, g3) for g3 in ((0, 1) if h == 0 else (2,))]):
                        pe.wait_ge(emptied[which].sem, count)
                    for i in range(4):
                        last = nc.tensor.transpose(b[:, i * P:(i + 1) * P], num_t[:, 4 * h + i, :], ident[:])
                elif kind == "PROJ":
                    ob, h = divmod(step[1], 2)
                    if step[1] == 0:
                        pe.wait_ge(wproj_in.sem, wproj_in.value(it, 0))
                        if not f[1]:
                            for i in range(BANKS):
                                pe.wait_ge(emptied[i].sem, emptied[i].value(it, 0))
                    for k in range(2 * SETS):
                        last = mm(b[:], wproj_sb[:, k, ob * P:(ob + 1) * P], feat[:, k, h * HALF:(h + 1) * HALF],
                                  start=(k == 0), stop=(k == 2 * SETS - 1))
                last.then_inc(product.sem, 1)

            def iteration(it, f):
                for step in STEPS[f]:
                    if step[0] in GROUPS:
                        group(it, f, step)
                    elif step[0] == "S":
                        n = step[1]
                        j, qb, hd = n // (2 * QB), n // 2 % QB, n % 2
                        if positive(exp_done.value(it, n - 1)):
                            pe.wait_ge(exp_done.sem, exp_done.value(it, n - 1))
                        if n % (2 * QB) < 2:
                            pe.wait_ge(twice_done.sem, twice_done.value(it, 2 * j + hd + 1))
                            pe.wait_ge(low_done.sem, low_done.value(it, 4 * j + 2 * hd + 2))
                        for h in range(2):
                            for part in range(2):
                                last = mm(scores[hd][:, h * HALF:(h + 1) * HALF], q_st[:, hd, qb * P:(qb + 1) * P],
                                          k_st[:, hd, part, h * HALF:(h + 1) * HALF],
                                          start=(part == 0), stop=(part == 1))
                        last.then_inc(scores_full.sem, 1)
                    elif step[0] == "TAPS":
                        _, m, h = step
                        if h == 0:
                            pe.wait_ge(diagonals_done, m + 1)
                            for which, count in copies(f, it, ("P1", m, 0), ("P1", m, 1)):
                                pe.wait_ge(emptied[which].sem, count)
                            if m >= 2:
                                pe.wait_ge(conv_step.sem, conv_step.value(it, (m - 1) * vector_steps(True)))
                        for i, tap in enumerate(BY_TENSOR):
                            ty, tx = divmod(tap, TAPS)
                            rows = slice(ty + h * H // 2, ty + (h + 1) * H // 2)
                            last = mm(scores[m % 2][:, h * HALF:(h + 1) * HALF], diagonal[:, m % 2, i, :],
                                      pads[m % 3][:, rows, tx:tx + W], start=(i == 0), stop=(i == len(BY_TENSOR) - 1))
                        last.then_inc(taps_full, 1)
                    elif step[0] in ("MEAN", "VAR"):
                        pe.wait_ge(stats_done.sem, stats_done.value(it, 1 if step[0] == "MEAN" else 2))
                        at = 0 if step[0] == "MEAN" else HALF
                        mm(scores[0][:, at:at + 1], mean_w[:], mv[:, 0:1] if step[0] == "MEAN" else gn[:, 1:2],
                           start=True, stop=True).then_inc(sums_full.sem, 1)

            iteration(0, BEGIN)
            iteration(1, SECOND)
            with pe.Fori(2, NB) as it:
                iteration(it, STEADY)
            iteration(NB, DRAIN)
            iteration(NB + 1, END)

        @block.scalar
        def _(act):
            act.wait_ge(const_in, 16 * 11)

            def fn(dst, src, func, **kw):
                return nc.scalar.activation(dst, src, func, **kw)

            def iteration(it, f):
                for step in STEPS[f]:
                    kind = step[0]
                    g = INDEX[f].get(step)
                    if kind == "EXP":
                        n = step[1]
                        act.wait_ge(max_done.sem, max_done.value(it, n + 1))
                        fn(exp_bias[:, n % 4:n % 4 + 1], neg_max[:, n % 4:n % 4 + 1], ACT.Copy, scale=CH ** -0.5)\
                            .then_inc(bias_done.sem, 1)
                        act.wait_ge(bias_done.sem, bias_done.value(it, n + 1))
                        if n < 2 and f[2]:
                            for sent in out_sent[2 * n:2 * n + 2]:
                                act.wait_ge(sent.sem, sent.value(it, 2 * CB // RING))
                        if n >= 2:
                            act.wait_ge(product.sem, products(f, it, ("T", n - 2, 1)))
                        fn(probs[n % 2][:], scores[n % 2][:], ACT.Exp, bias=exp_bias[:, n % 4:n % 4 + 1],
                           scale=CH ** -0.5, accum_out=row_sum[:, n % 16:n % 16 + 1]).then_inc(exp_done.sem, 1)
                    elif kind == "T":
                        _, n, h = step
                        act.wait_ge(product.sem, products(f, it, step))
                        fn(pt[:, n % 2, 4 * h:4 * h + 4, n // 2 % 2 * P:(n // 2 % 2 + 1) * P],
                           bank[g % BANKS][:].rearrange("p (a b) -> p a b", b=P), ACT.Copy)\
                            .then_inc(emptied[g % BANKS].sem, 1)
                    elif kind == "WIDE":
                        c = step[1]
                        act.wait_ge(inv_done.sem, inv_done.value(it, c + 1))
                        fn(inv_wide[:], inv_sum[:, c % 2, :].unsqueeze(2).broadcast_to((P, 4, CH)), ACT.Copy)\
                            .then_inc(wide_done.sem, 1)
                    elif kind == "COPY" and step[1][0] == "AV":
                        c = step[1][1]
                        g = INDEX[f][step[1]]
                        act.wait_ge(product.sem, products(f, it, step[1]))
                        fn(vy[:, c // 4, c % 4 * 2 * P:(c % 4 + 1) * 2 * P], bank[g % BANKS][:, 0:2 * P], ACT.Copy)\
                            .then_inc(emptied[g % BANKS].sem, 1)
                    elif kind == "SPREAD":
                        c = step[1]
                        act.wait_ge(product.sem, products(f, it, step))
                        if positive(norm_done.value(it, c)):
                            act.wait_ge(norm_done.sem, norm_done.value(it, c))
                        fn(inv_q[:], bank[g % BANKS][:, 0:2 * P], ACT.Copy).then_inc(emptied[g % BANKS].sem, 1)
                    elif kind == "VAR":
                        act.wait_ge(affine_done.sem, affine_done.value(it, 1))
                        for k in range(CB):
                            last = fn(u[:, k, :], u[:, k, :], ACT.Identity, scale=gn_a[:, k:k + 1],
                                      bias=gn_nb[:, k:k + 1])
                        last.then_inc(u_ready.sem, 1)
                    elif kind == "V":
                        act.wait_ge(product.sem, products(f, it, step))
                        tb = step[1]
                        fn(vy[:, 1:PAIRS + 1, tb * P:(tb + 1) * P],
                           bank[g % BANKS][:].rearrange("p (j c) -> p j c", j=PAIRS), ACT.Copy)\
                            .then_inc(emptied[g % BANKS].sem, 1)
                    elif kind == "QK":
                        _, j, t, h = step
                        act.wait_ge(product.sem, products(f, it, step))
                        fn(qk_raw[:, t, h * HALF:(h + 1) * HALF], bank[g % BANKS][:], ACT.Identity,
                           bias=qkb_sb[:, j, t:t + 1]).then_inc(emptied[g % BANKS].sem, 1)
                    elif kind == "HIGH":
                        _, j, hd = step
                        if hd == 0:
                            if positive(scores_full.value(it, 2 * QB * j)):
                                act.wait_ge(scores_full.sem, scores_full.value(it, 2 * QB * j))
                            for which, count in copies(f, it, *[("QK", j, t, h) for t in range(2) for h in range(2)]):
                                act.wait_ge(emptied[which].sem, count)
                        rows = slice(hd * CH, (hd + 1) * CH)
                        fn(k_st[0:CH, hd, 0, :], qk_raw[rows, 1, :], ACT.Copy).then_inc(high_done.sem, 1)
                        fn(q_st[0:CH, hd, :], qk_raw[rows, 0, :], ACT.Copy).then_inc(high_done.sem, 1)
                        fn(k_st[CH:P, hd, 0, :], qk_raw[rows, 1, :], ACT.Copy)
                    elif kind == "TWICE":
                        _, j, hd = step
                        act.wait_ge(low_done.sem, low_done.value(it, 4 * j + 2 * hd + 1))
                        fn(k_st[CH:P, hd, 1, :], k_st[0:CH, hd, 1, :].bitcast(F32), ACT.Copy)\
                            .then_inc(twice_done.sem, 1)
                    elif kind == "P1":
                        _, m, h = step
                        t = m % 3
                        act.wait_ge(product.sem, products(f, it, step))
                        if m == BLOCKS - 1 and f[0]:
                            act.wait_ge(x1_sent.sem, x1_sent.value(it, 0))
                        if m >= 3:
                            act.wait_ge(conv_step.sem, conv_step.value(it, (m - 2) * vector_steps(f == DRAIN)))
                        rows = slice(PAD + h * H // 2, PAD + (h + 1) * H // 2)
                        src = bank[g % BANKS][:]
                        fn(pads[m % 3][:, rows, PAD:PAD + W], src.rearrange("p (a b) -> p a b", b=W), ACT.Copy)
                        dst = q_orig if t == 0 else kv_raw
                        fn(dst[:, h * HALF:(h + 1) * HALF], src, ACT.Copy if t == 2 else ACT.Relu)\
                            .then_inc(emptied[g % BANKS].sem, 1)
                        if h == 1:
                            for which, count in copies(f, it, ("P1", m, 0), ("P1", m, 1)):
                                act.wait_ge(emptied[which].sem, count)
                            if m >= 2:
                                act.wait_ge(product.sem, products(f, it, ("PW", m - 2, 1)))
                            if f == DRAIN:
                                if m >= 2:
                                    act.wait_ge(taps_full, 2 * (m - 1))
                                for i, tap in enumerate(BY_TENSOR):
                                    last = fn(diagonal[:, m % 2, i, :], ident[:], ACT.Copy,
                                              scale=dw_sb[:, m, tap:tap + 1])
                                last.then_inc(diagonals_done, 1)
                            ty, tx = divmod(BY_SCALAR, TAPS)
                            fn(acc[m % 2][:], pads[m % 3][:, ty:ty + H, tx:tx + W], ACT.Copy,
                               scale=dw_sb[:, m, BY_SCALAR:BY_SCALAR + 1]).then_inc(tap_done.sem, 1)
                    elif kind in ("PW", "TK", "TV", "TB"):
                        act.wait_ge(product.sem, products(f, it, step))
                        src = bank[g % BANKS][:]
                        h = step[-1]
                        cols = slice(h * HALF, (h + 1) * HALF)
                        src3 = src.rearrange("p (a b) -> p a b", b=P)
                        what = step[1] % 3 if kind == "PW" else {"TK": 1, "TV": 2, "TB": 3}[kind]
                        if what == 0:
                            last = fn(q_agg[:, cols], src, ACT.Relu)
                        elif what == 1:
                            last = fn(k_t[:, 4 * h:4 * h + 4, :], src3, ACT.Relu)
                        elif what == 2:
                            last = fn(v_t[:, 4 * h:4 * h + 4, 0:P], src3, ACT.Copy)
                        else:
                            last = fn(feat[:, SETS * step[1] + step[2], cols], src, ACT.Copy)
                        last.then_inc(emptied[g % BANKS].sem, 1)
                    elif step[0] == "COPY" and step[1][0] == "PROJ":
                        i = step[1][1]
                        ob, h = divmod(i, 2)
                        for which, count in copies(f, it, step[1]):
                            act.wait_ge(emptied[which].sem, count)
                        dst = out[bass.ds(it - 2, 1)] if not isinstance(it, int) else out[it - 2:it - 1]
                        dst = dst[:, ob * P:(ob + 1) * P, h * HALF:(h + 1) * HALF]
                        act.dma_start(dst.rearrange("a p t -> (a p) t"), part[i % RING])\
                            .then_inc(out_sent[i % RING].sem, 16)
                    elif step == ("COPY", ("OUT", 2 * CB - 1)):
                        for which, count in copies(f, it, ("OUT", 2 * CB - 2), ("OUT", 2 * CB - 1)):
                            act.wait_ge(emptied[which].sem, count)
                        dst = x1_dram[bass.ds(it, 1)] if not isinstance(it, int) else x1_dram[it:it + 1]
                        act.dma_start(dst.rearrange("a (k p) t -> p (a k) t", p=P), x1[:]).then_inc(x1_sent.sem, 16)
                if not f[0] and f[2]:
                    for sent in out_sent:
                        act.wait_ge(sent.sem, sent.value(it, 2 * CB // RING))

            iteration(0, BEGIN)
            iteration(1, SECOND)
            with act.Fori(2, NB) as it:
                iteration(it, STEADY)
            iteration(NB, DRAIN)
            iteration(NB + 1, END)

        @block.gpsimd
        def _(pool):
            pool.wait_ge(setup_dve, 1)
            with pool.Fori(0, NB) as it:
                pool.wait_ge(var_done.sem, it + 1)
                nc.gpsimd.tensor_tensor(gn[:, 3:4], gn[:, 4:5], gn[:, 5:6], ALU.pow).then_inc(std_done.sem, 1)

        @block.vector
        def _(dve):
            v = nc.vector
            for p in pads:
                v.memset(p[:], 0.0)
            v.memset(gn[:, 5:6], -0.5)
            v.memset(v_t[:, :, P:P + 1], 1.0).then_inc(setup_dve, 1)
            dve.wait_ge(const_in, 16 * 11)
            for m in range(BLOCKS):
                last = v.tensor_tensor(pw_bd[:, m, :].rearrange("p (h c) -> p h c", c=DIM),
                                       pw_dense[:, m, :].unsqueeze(1).broadcast_to((P, HEADS_SET, DIM)),
                                       bdmask[:].rearrange("p (h c) -> p h c", c=DIM), ALU.mult)
            last.then_inc(setup_dve, 1)
            dve.wait_ge(setup_pe, 1)
            v.tensor_tensor(outb2[:], scores[0][:, 0:CB], outb_sb[:], ALU.add).then_inc(setup_dve, 1)
            dve.wait_ge(setup_dve, 3)

            def iteration(it, f):
                links = [0]

                def link(ins):
                    links[0] += 1
                    ins.then_inc(link_done.sem, 1)
                    dve.wait_ge(link_done.sem, link_done.value(it, links[0]))

                for step in STEPS[f]:
                    if step[0] in BY_VECTOR or step[0] == "COPY" and step[1][0] not in BY_VECTOR:
                        continue
                    if step[0] == "COPY":
                        step = step[1]
                    kind = step[0]
                    g = INDEX[f].get(step)
                    if kind == "MAX":
                        n = step[1]
                        dve.wait_ge(scores_full.sem, scores_full.value(it, n + 1))
                        v.tensor_reduce(neg_max[:, n % 4:n % 4 + 1], scores[n % 2][:], AX_X, ALU.max, negate=True)\
                            .then_inc(max_done.sem, 1)
                    elif kind == "CONV":
                        _, m, i = step
                        if i == BY_SCALAR:
                            continue
                        if i == 0:
                            for which, count in copies(f, it, ("P1", m, 0), ("P1", m, 1)):
                                dve.wait_ge(emptied[which].sem, count)
                        taps, per_block = vector_taps(f == DRAIN), vector_steps(f == DRAIN)
                        full = acc[m % 2]
                        if i == TAP_STEPS:
                            at = m * per_block + len(taps)
                            dve.wait_ge(conv_step.sem, conv_step.value(it, at))
                            v.tensor_tensor(full[:], full[:], side[:], ALU.add).then_inc(conv_step.sem, 1)
                            if f == DRAIN:
                                dve.wait_ge(conv_step.sem, conv_step.value(it, at + 1))
                                dve.wait_ge(taps_full, 2 * m + 2)
                                v.tensor_tensor(full[:], full[:], scores[m % 2][:].rearrange("p (a b) -> p a b", b=W),
                                                ALU.add).then_inc(conv_step.sem, 1)
                            continue
                        if i not in taps:
                            continue
                        dst = (full, side)[CHAIN[i]]
                        ty, tx = divmod(i, TAPS)
                        src = pads[m % 3][:, ty:ty + H, tx:tx + W]
                        wt = dw_sb[:, m, i:i + 1]
                        before = [k for k in taps + [BY_SCALAR] if k < i and CHAIN[k] == CHAIN[i]]
                        if before:
                            if max(before) == BY_SCALAR:
                                dve.wait_ge(tap_done.sem, tap_done.value(it, m + 1))
                            else:
                                done = taps.index(max(before)) + 1
                                dve.wait_ge(conv_step.sem, conv_step.value(it, m * per_block + done))
                            v.scalar_tensor_tensor(dst[:], src, wt, dst[:], ALU.mult, ALU.add)\
                                .then_inc(conv_step.sem, 1)
                        else:
                            if m > 0:
                                done = m * per_block - (1 if f == DRAIN else 0)
                                dve.wait_ge(conv_step.sem, conv_step.value(it, done))
                            v.tensor_scalar(dst[:], src, wt, None, ALU.mult).then_inc(conv_step.sem, 1)
                    elif kind == "STATS":
                        dve.wait_ge(x_in.sem, x_in.value(it, 1))
                        for i in range(2 * CB):
                            last = v.bn_stats(bn6[:, i, :], u[:, i // 2, i % 2 * HALF:(i % 2 + 1) * HALF])
                        link(last)
                        v.tensor_copy(gn[:, 6:7], gn[:, 5:6])
                        v.bn_aggr(mv[:], bn6[:].rearrange("p a b -> p (a b)")).then_inc(stats_done.sem, 1)
                    elif kind == "MEAN":
                        dve.wait_ge(sums_full.sem, sums_full.value(it, 1))
                        ps = scores[0][:, 0:1]
                        link(v.tensor_tensor(gn[:, 0:1], mv[:, 0:1], ps, ALU.subtract))
                        v.tensor_copy(gn[:, 2:3], ps)
                        v.tensor_scalar(gn[:, 1:2], gn[:, 0:1], gn[:, 0:1], mv[:, 1:2], ALU.mult, ALU.add)\
                            .then_inc(stats_done.sem, 1)
                    elif kind == "VAR":
                        dve.wait_ge(sums_full.sem, sums_full.value(it, 2))
                        v.tensor_scalar(gn[:, 4:5], scores[0][:, HALF:HALF + 1], GN_EPS, None, ALU.add)\
                            .then_inc(var_done.sem, 1)
                        dve.wait_ge(std_done.sem, std_done.value(it, 1))
                        link(v.tensor_scalar(gn_a[:], gnw_sb[:], gn[:, 3:4], None, ALU.mult))
                        link(v.tensor_scalar(gn_nb[:], gn_a[:], gn[:, 2:3], None, ALU.mult))
                        v.tensor_tensor(gn_nb[:], gnb_sb[:], gn_nb[:], ALU.subtract).then_inc(affine_done.sem, 1)
                    elif kind == "LOW":
                        _, j, hd = step
                        rows = slice(hd * CH, (hd + 1) * CH)
                        dve.wait_ge(high_done.sem, high_done.value(it, 4 * j + 2 * hd + 1))
                        v.tensor_tensor(k_st[0:CH, hd, 1, :], qk_raw[rows, 1, :],
                                        k_st[0:CH, hd, 0, :].bitcast(F32), ALU.subtract).then_inc(low_done.sem, 1)
                        dve.wait_ge(high_done.sem, high_done.value(it, 4 * j + 2 * hd + 2))
                        v.tensor_tensor(q_st[CH:P, hd, :], qk_raw[rows, 0, :],
                                        q_st[0:CH, hd, :].bitcast(F32), ALU.subtract).then_inc(low_done.sem, 1)
                    elif kind == "RECIP":
                        c = step[1]
                        dve.wait_ge(exp_done.sem, exp_done.value(it, 4 * c + 4))
                        v.reciprocal(inv_sum[:, c % 2, :], row_sum[:, 4 * c % 16:4 * c % 16 + 4])\
                            .then_inc(inv_done.sem, 1)
                    elif kind == "NORM":
                        c = step[1]
                        for which, count in copies(f, it, ("AV", c), ("SPREAD", c)):
                            dve.wait_ge(emptied[which].sem, count)
                        y = vy[:, c // 4, c % 4 * 2 * P:(c % 4 + 1) * 2 * P]
                        v.tensor_tensor(y, y, inv_q[:], ALU.mult).then_inc(norm_done.sem, 1)
                    elif kind == "VK":
                        dve.wait_ge(product.sem, products(f, it, step))
                        ps = bank[g % BANKS]
                        v.tensor_tensor(vk[:, 0:P], ps[:, 0:P], bdmask[:], ALU.mult)
                        v.tensor_scalar(vk[:, P:NW], hmask[:], ps[:, P:P + 1], None, ALU.mult)\
                            .then_inc(emptied[g % BANKS].sem, 1)
                    elif kind == "NUM":
                        _, s, j, g3 = step
                        dve.wait_ge(product.sem, products(f, it, step))
                        nb = min(QB, 3 * g3 + 3) - 3 * g3
                        ps = bank[g % BANKS][:, 0:nb * NW].rearrange("p (a b) -> p a b", b=NW)
                        d = [den[:, g % 2, i, 0:nb * HEADS_SET].rearrange("p (a b) -> p a b", b=HEADS_SET)
                             for i in range(2)]
                        link(v.tensor_scalar(d[0], ps[:, :, P:NW], ATT_EPS, None, ALU.add))
                        link(v.reciprocal(d[1], d[0]))
                        v.tensor_tensor(num_t[:, 3 * g3:3 * g3 + nb, :].rearrange("p a (h c) -> p a h c", c=DIM),
                                        ps[:, :, 0:P].rearrange("p a (h c) -> p a h c", c=DIM),
                                        d[1].unsqueeze(3).broadcast_to((P, nb, HEADS_SET, DIM)), ALU.mult)\
                            .then_inc(emptied[g % BANKS].sem, 1)
                    elif kind == "PROJ":
                        i = step[1]
                        ob, h = divmod(i, 2)
                        dve.wait_ge(product.sem, products(f, it, step))
                        dve.wait_ge(res_in[i % RING].sem, res_in[i % RING].value(it, i // RING + 1))
                        v.tensor_tensor(part[i % RING], bank[g % BANKS][:], part[i % RING], ALU.add)\
                            .then_inc(emptied[g % BANKS].sem, 1)
                    elif kind == "OUT":
                        h, ob = divmod(step[1], CB)
                        dve.wait_ge(product.sem, products(f, it, step))
                        if step[1] == 0:
                            dve.wait_ge(x_again_in.sem, x_again_in.value(it, 1))
                        cols = slice(h * HALF, (h + 1) * HALF)
                        v.scalar_tensor_tensor(x1[:, ob, cols], bank[g % BANKS][:], outb2[:, ob:ob + 1],
                                               x1[:, ob, cols], ALU.add, ALU.add).then_inc(emptied[g % BANKS].sem, 1)
                assert links[0] == (LINKS0 if f[0] else 0) + (LINKS1 if f[1] else 0), links

            iteration(0, BEGIN)
            iteration(1, SECOND)
            with dve.Fori(2, NB) as it:
                iteration(it, STEADY)
            iteration(NB, DRAIN)
            iteration(NB + 1, END)


def kernel(x, L0_conv_gn_weight, L0_conv_gn_bias, L0_conv_qkv_w, L0_conv_qkv_b, L0_conv_out_w, L0_conv_out_b,
           L1_conv_w_qkv, L1_conv_w_dw, L1_conv_w_pw, L1_conv_w_proj):
    import concourse.bacc as bacc
    from concourse.bass_utils import run_bass_kernel_spmd

    def lay(a):
        return np.ascontiguousarray(a)

    def per_block(a):
        return lay(np.asarray(a).reshape(-1, P).T)

    x, qkv_w, qkv_b = np.asarray(x), np.asarray(L0_conv_qkv_w), np.asarray(L0_conv_qkv_b)
    w_t = qkv_w.T.reshape(CB, P, 3, PAIRS, P)
    order = np.arange(3 * C).reshape(SETS, HEADS_SET, 3, DIM).transpose(0, 2, 1, 3).reshape(-1)
    w1 = np.asarray(L1_conv_w_qkv).reshape(3 * C, C)[order].reshape(SETS, 3, P, CB, P)
    arrays = {
        "x": lay(x.reshape(NB, C, L)),
        "w0qk": lay(w_t[:, :, 0:2].transpose(3, 1, 0, 2, 4)),
        "w0v": lay(w_t[:, :, 2].reshape(CB, P, C).transpose(1, 0, 2)),
        "w0out": lay(np.asarray(L0_conv_out_w).T.reshape(CB, P, C).transpose(1, 0, 2)),
        "w1": lay(w1.transpose(0, 4, 3, 1, 2)),
        "wproj": lay(np.asarray(L1_conv_w_proj).reshape(C, 2 * C).T.reshape(2 * SETS, P, C).transpose(1, 0, 2)),
        "pw": lay(np.asarray(L1_conv_w_pw).reshape(3 * C, DIM)[order].reshape(BLOCKS, HEADS_SET, DIM, DIM)
                  .transpose(1, 3, 0, 2).reshape(P, BLOCKS, DIM)),
        "dw": lay(np.asarray(L1_conv_w_dw).reshape(3 * C, TAPS * TAPS)[order].reshape(BLOCKS, P, -1)
                  .transpose(1, 0, 2)),
        "gnw": per_block(L0_conv_gn_weight),
        "gnb": per_block(L0_conv_gn_bias),
        "qk_bias": lay(qkv_b[:2 * C].reshape(2, PAIRS, P).transpose(2, 1, 0)),
        "v_bias": per_block(qkv_b[2 * C:]),
        "out_bias": per_block(L0_conv_out_b),
        "identity": np.eye(P, dtype=np.float32),
        "block_mask": np.kron(np.eye(HEADS_SET), np.ones((DIM, DIM))).astype(np.float32),
        "head_mask": np.kron(np.eye(HEADS_SET), np.ones((DIM, 1))).astype(np.float32),
        "ones": np.full((P, P), 1.0 / P, np.float32),
    }
    nc = bacc.Bacc("TRN2", target_bir_lowering=False, num_devices=1, dynamic_dma_scratch_size=1024)
    args = {n: nc.dram_tensor(f"in_{n}", a.shape, F32, kind="ExternalInput").ap() for n, a in arrays.items()}
    out = nc.dram_tensor("out_0", (NB, C, L), F32, kind="ExternalOutput").ap()
    build(nc, out=out, **args)
    r = run_bass_kernel_spmd(nc, [{f"in_{n}": a for n, a in arrays.items()}], core_ids=[0])
    return r.results[0]["out_0"].reshape(NB, C, H, W)
```
